# Optimizing a Trainium2 kernel written in Bass

```python
import numpy as np
import jax
import jax.numpy as jnp

def _softmax(x, axis=-1):
    return jax.nn.softmax(x, axis=axis)

def _gelu(x):
    return jax.nn.gelu(x, approximate=True)

def _silu(x):
    return jax.nn.silu(x)

def _sigmoid(x):
    return jax.nn.sigmoid(x)

def _layernorm(x, axis=-1, eps=1e-05):
    m = jnp.mean(x, axis=axis, keepdims=True)
    v = jnp.var(x, axis=axis, keepdims=True)
    return (x - m) / jnp.sqrt(v + eps)

def _scatter_add(tgt, idx, src, axis=0):
    return tgt.at[idx].add(src)

def _segment_sum(src, seg, n):
    return jax.ops.segment_sum(src, seg, n)
kernel_name = 'mk_sandwich_d2_jaxref_r8_1ccd9b'

def setup_inputs(seed: int=0):
    np.random.seed(seed)
    _w = jnp.asarray

    def _L0_attn_setup():
        import jax, jax.numpy as jnp
        import numpy as np
        DIM = 256
        HEADS = 16
        HEAD_DIM = DIM // HEADS
        RANK = 16
        ALPHA = 8.0
        SCALING = ALPHA / RANK
        SCALE = HEAD_DIM ** (-0.5)

        def lora_linear(x, W, b, Bm, Am):
            out = jnp.einsum('bld,od->blo', x, W) + b
            upd = jnp.einsum('blr,or->blo', jnp.einsum('bld,rd->blr', x, Bm), Am)
            return out + SCALING * upd

        def _split(t):
            B, L, D = t.shape
            return t.reshape(B, L, HEADS, HEAD_DIM).transpose(0, 2, 1, 3)
        key = jax.random.key(seed)
        ks = jax.random.split(key, 20)
        B, L = (4, 256)
        x = jax.random.normal(ks[0], (B, L, DIM), dtype=jnp.float32)
        s = 0.02
        inp = {'x': x}
        for i, name in enumerate(['q', 'k', 'v', 'o']):
            inp[f'W{name}'] = jax.random.normal(ks[1 + 4 * i], (DIM, DIM), jnp.float32) * s
            inp[f'b{name}'] = jax.random.normal(ks[2 + 4 * i], (DIM,), jnp.float32) * s
            inp[f'B{name}'] = jax.random.normal(ks[3 + 4 * i], (RANK, DIM), jnp.float32) * s
            inp[f'A{name}'] = jax.random.uniform(ks[4 + 4 * i], (DIM, RANK), jnp.float32, -0.1, 0.1)
        return inp
    _L0_attn_in = _L0_attn_setup()

    def _L0_ffn_setup():
        import jax, jax.numpy as jnp
        import numpy as np
        H = 256
        I = 1024
        NE = 8
        S = 2
        N = NE - S
        K = N
        E = I // NE
        C = 2
        RESIDUAL = True
        B, L = (2, 256)

        def _swiglu(h, W, b):
            return jax.nn.silu(h @ W + b) * h
        key = jax.random.key(seed)
        ks = jax.random.split(key, 16)
        s = 0.02
        inp = {'x': jax.random.normal(ks[0], (B, L, H), dtype=jnp.float32), 'Wg': jax.random.normal(ks[1], (C, H, NE)) * s, 'bg': jnp.zeros((C, NE)), 'Wup': jax.random.normal(ks[2], (N, H, E)) * s, 'bup': jnp.zeros((N, E)), 'Wsw': jax.random.normal(ks[3], (N, E, E)) * s, 'bsw': jnp.zeros((N, E)), 'Wdn': jax.random.normal(ks[4], (N, E, H)) * s, 'bdn': jnp.zeros((N, H)), 'Wsu': jax.random.normal(ks[5], (H, S * E)) * s, 'bsu': jnp.zeros((S * E,)), 'Wsa': jax.random.normal(ks[6], (E, E)) * s, 'bsa': jnp.zeros((E,)), 'Wsd': jax.random.normal(ks[7], (S * E, H)) * s, 'bsd': jnp.zeros((H,))}
        return inp
    _L0_ffn_in = _L0_ffn_setup()

    def _L1_attn_setup():
        import jax, jax.numpy as jnp
        import numpy as np
        N_HEAD = 16
        N_KV_HEAD = 4
        N_EMBD = 256

        def rotate_half(x):
            x1, x2 = jnp.split(x, 2, axis=-1)
            return jnp.concatenate([-x2, x1], axis=-1)

        def rope_tables(T, k):
            inv = jnp.power(10000.0, -2.0 * jnp.arange(k // 2, dtype=jnp.float32) / k)
            ang = jnp.arange(T, dtype=jnp.float32)[:, None] * inv[None, :]
            cos = jnp.tile(jnp.cos(ang), (1, 2))
            sin = jnp.tile(jnp.sin(ang), (1, 2))
            return (cos, sin)
        key = jax.random.key(seed)
        ks = jax.random.split(key, 5)
        B, T, D = (4, 128, N_EMBD)
        g, h = (N_KV_HEAD, N_HEAD)
        k = D // h
        s = 0.02
        return {'x': jax.random.normal(ks[0], (B, T, D), dtype=jnp.float32), 'Wq': jax.random.normal(ks[1], (D, D), dtype=jnp.float32) * s, 'Wk': jax.random.normal(ks[2], (D, g * k), dtype=jnp.float32) * s, 'Wv': jax.random.normal(ks[3], (D, g * k), dtype=jnp.float32) * s, 'Wo': jax.random.normal(ks[4], (D, D), dtype=jnp.float32) * s}
    _L1_attn_in = _L1_attn_setup()

    def _L1_ffn_setup():
        import jax, jax.numpy as jnp
        import numpy as np
        TOP_P = 0.9
        S, B, H, I, E = (256, 4, 256, 512, 8)

        def _top_p_weights(probs, top_p):
            order = jnp.argsort(-probs, axis=-1)
            sp = jnp.take_along_axis(probs, order, axis=-1)
            cum = jnp.cumsum(sp, axis=-1)
            exceed = cum > top_p
            first_idx = jnp.argmax(exceed, axis=-1)
            first = jnp.arange(probs.shape[-1])[None, :] == first_idx[:, None]
            keep = ~exceed | first
            kept = jnp.where(keep, sp, 0.0)
            t_idx = jnp.arange(probs.shape[0])[:, None]
            return jnp.zeros_like(probs).at[t_idx, order].set(kept)
        key = jax.random.key(seed)
        ks = jax.random.split(key, 5)
        scale = 0.02
        return {'hidden_states': jax.random.normal(ks[0], (S, B, H), dtype=jnp.float32), 'router_w': jax.random.normal(ks[1], (E, H), dtype=jnp.float32) * scale, 'gate_w': jax.random.normal(ks[2], (E, I, H), dtype=jnp.float32) * scale, 'up_w': jax.random.normal(ks[3], (E, I, H), dtype=jnp.float32) * scale, 'down_w': jax.random.normal(ks[4], (E, H, I), dtype=jnp.float32) * scale}
    _L1_ffn_in = _L1_ffn_setup()
    _d = {'L0_attn_x': _L0_attn_in['x'], 'L0_attn_Wq': _L0_attn_in['Wq'], 'L0_attn_bq': _L0_attn_in['bq'], 'L0_attn_Bq': _L0_attn_in['Bq'], 'L0_attn_Aq': _L0_attn_in['Aq'], 'L0_attn_Wk': _L0_attn_in['Wk'], 'L0_attn_bk': _L0_attn_in['bk'], 'L0_attn_Bk': _L0_attn_in['Bk'], 'L0_attn_Ak': _L0_attn_in['Ak'], 'L0_attn_Wv': _L0_attn_in['Wv'], 'L0_attn_bv': _L0_attn_in['bv'], 'L0_attn_Bv': _L0_attn_in['Bv'], 'L0_attn_Av': _L0_attn_in['Av'], 'L0_attn_Wo': _L0_attn_in['Wo'], 'L0_attn_bo': _L0_attn_in['bo'], 'L0_attn_Bo': _L0_attn_in['Bo'], 'L0_attn_Ao': _L0_attn_in['Ao'], 'L0_ffn_Wg': _L0_ffn_in['Wg'], 'L0_ffn_bg': _L0_ffn_in['bg'], 'L0_ffn_Wup': _L0_ffn_in['Wup'], 'L0_ffn_bup': _L0_ffn_in['bup'], 'L0_ffn_Wsw': _L0_ffn_in['Wsw'], 'L0_ffn_bsw': _L0_ffn_in['bsw'], 'L0_ffn_Wdn': _L0_ffn_in['Wdn'], 'L0_ffn_bdn': _L0_ffn_in['bdn'], 'L0_ffn_Wsu': _L0_ffn_in['Wsu'], 'L0_ffn_bsu': _L0_ffn_in['bsu'], 'L0_ffn_Wsa': _L0_ffn_in['Wsa'], 'L0_ffn_bsa': _L0_ffn_in['bsa'], 'L0_ffn_Wsd': _L0_ffn_in['Wsd'], 'L0_ffn_bsd': _L0_ffn_in['bsd'], 'L1_attn_Wq': _L1_attn_in['Wq'], 'L1_attn_Wk': _L1_attn_in['Wk'], 'L1_attn_Wv': _L1_attn_in['Wv'], 'L1_attn_Wo': _L1_attn_in['Wo'], 'L1_ffn_router_w': _L1_ffn_in['router_w'], 'L1_ffn_gate_w': _L1_ffn_in['gate_w'], 'L1_ffn_up_w': _L1_ffn_in['up_w'], 'L1_ffn_down_w': _L1_ffn_in['down_w']}
    _x0 = _d['L0_attn_x']
    _d['L0_attn_x'] = jax.random.normal(jax.random.fold_in(jax.random.key(seed), 1), (1, 1024, 256), dtype=_x0.dtype)
    del _x0
    return _d

def reference(L0_attn_x, L0_attn_Wq, L0_attn_bq, L0_attn_Bq, L0_attn_Aq, L0_attn_Wk, L0_attn_bk, L0_attn_Bk, L0_attn_Ak, L0_attn_Wv, L0_attn_bv, L0_attn_Bv, L0_attn_Av, L0_attn_Wo, L0_attn_bo, L0_attn_Bo, L0_attn_Ao, L0_ffn_Wg, L0_ffn_bg, L0_ffn_Wup, L0_ffn_bup, L0_ffn_Wsw, L0_ffn_bsw, L0_ffn_Wdn, L0_ffn_bdn, L0_ffn_Wsu, L0_ffn_bsu, L0_ffn_Wsa, L0_ffn_bsa, L0_ffn_Wsd, L0_ffn_bsd, L1_attn_Wq, L1_attn_Wk, L1_attn_Wv, L1_attn_Wo, L1_ffn_router_w, L1_ffn_gate_w, L1_ffn_up_w, L1_ffn_down_w):

    def _L0_attn_ref(x, Wq, bq, Bq, Aq, Wk, bk, Bk, Ak, Wv, bv, Bv, Av, Wo, bo, Bo, Ao):
        import jax, jax.numpy as jnp
        import numpy as np
        DIM = 256
        HEADS = 16
        HEAD_DIM = DIM // HEADS
        RANK = 16
        ALPHA = 8.0
        SCALING = ALPHA / RANK
        SCALE = HEAD_DIM ** (-0.5)

        def lora_linear(x, W, b, Bm, Am):
            out = jnp.einsum('bld,od->blo', x, W) + b
            upd = jnp.einsum('blr,or->blo', jnp.einsum('bld,rd->blr', x, Bm), Am)
            return out + SCALING * upd

        def _split(t):
            B, L, D = t.shape
            return t.reshape(B, L, HEADS, HEAD_DIM).transpose(0, 2, 1, 3)
        q = _split(lora_linear(x, Wq, bq, Bq, Aq))
        k = _split(lora_linear(x, Wk, bk, Bk, Ak))
        v = _split(lora_linear(x, Wv, bv, Bv, Av))
        scores = jnp.einsum('bhqd,bhkd->bhqk', q, k) * SCALE
        attn = jax.nn.softmax(scores, axis=-1)
        out = jnp.einsum('bhqk,bhkd->bhqd', attn, v)
        B, H, L, hd = out.shape
        out = out.transpose(0, 2, 1, 3).reshape(B, L, H * hd)
        return lora_linear(out, Wo, bo, Bo, Ao)

    def _L0_ffn_ref(x, Wg, bg, Wup, bup, Wsw, bsw, Wdn, bdn, Wsu, bsu, Wsa, bsa, Wsd, bsd):
        import jax, jax.numpy as jnp
        import numpy as np
        H = 256
        I = 1024
        NE = 8
        S = 2
        N = NE - S
        K = N
        E = I // NE
        C = 2
        RESIDUAL = True
        B, L = (2, 256)

        def _swiglu(h, W, b):
            return jax.nn.silu(h @ W + b) * h
        bsz, seq, _ = x.shape
        xt = x.reshape(-1, H)
        res = xt
        for j in range(C):
            gate = xt @ Wg[j] + bg[j]
            _, ids = jax.lax.top_k(gate, K)
            in_top = jax.nn.one_hot(ids, NE, dtype=gate.dtype).sum(-2) > 0
            w = jax.nn.softmax(jnp.where(in_top, gate, -jnp.inf), axis=-1)
            h = jnp.einsum('th,nhe->nte', xt, Wup) + bup[:, None, :]
            h = jax.nn.silu(jnp.einsum('nte,nef->ntf', h, Wsw) + bsw[:, None, :]) * h
            eo = jnp.einsum('nte,neh->nth', h, Wdn) + bdn[:, None, :]
            out = jnp.einsum('nth,tn->th', eo, w[:, :N])
            sh = (xt @ Wsu + bsu).reshape(-1, S, E)
            sh = _swiglu(sh, Wsa, bsa)
            out = out + sh.reshape(-1, S * E) @ Wsd + bsd
            xt = res + out if RESIDUAL else out
        return xt.reshape(bsz, seq, H)

    def _L1_attn_ref(x, Wq, Wk, Wv, Wo):
        import jax, jax.numpy as jnp
        import numpy as np
        N_HEAD = 16
        N_KV_HEAD = 4
        N_EMBD = 256

        def rotate_half(x):
            x1, x2 = jnp.split(x, 2, axis=-1)
            return jnp.concatenate([-x2, x1], axis=-1)

        def rope_tables(T, k):
            inv = jnp.power(10000.0, -2.0 * jnp.arange(k // 2, dtype=jnp.float32) / k)
            ang = jnp.arange(T, dtype=jnp.float32)[:, None] * inv[None, :]
            cos = jnp.tile(jnp.cos(ang), (1, 2))
            sin = jnp.tile(jnp.sin(ang), (1, 2))
            return (cos, sin)
        B, T, D = x.shape
        h, g = (N_HEAD, N_KV_HEAD)
        k = D // h
        Q = (x @ Wq).reshape(B, T, h, k).transpose(0, 2, 1, 3)
        K = (x @ Wk).reshape(B, T, g, k).transpose(0, 2, 1, 3)
        V = (x @ Wv).reshape(B, T, g, k).transpose(0, 2, 1, 3)
        K = jnp.repeat(K, h // g, axis=1)
        V = jnp.repeat(V, h // g, axis=1)
        cos, sin = rope_tables(T, k)
        cos = cos[None, None]
        sin = sin[None, None]
        Q = Q * cos + rotate_half(Q) * sin
        K = K * cos + rotate_half(K) * sin
        scores = jnp.einsum('bhqk,bhsk->bhqs', Q, K) / jnp.sqrt(jnp.float32(k))
        causal = jnp.tril(jnp.ones((T, T), dtype=bool))
        scores = jnp.where(causal[None, None], scores, -jnp.inf)
        A = jax.nn.softmax(scores, axis=-1)
        Y = jnp.einsum('bhqs,bhsk->bhqk', A, V)
        Y = Y.transpose(0, 2, 1, 3).reshape(B, T, D)
        return Y @ Wo

    def _L1_ffn_ref(hidden_states, router_w, gate_w, up_w, down_w):
        import jax, jax.numpy as jnp
        import numpy as np
        TOP_P = 0.9
        S, B, H, I, E = (256, 4, 256, 512, 8)

        def _top_p_weights(probs, top_p):
            order = jnp.argsort(-probs, axis=-1)
            sp = jnp.take_along_axis(probs, order, axis=-1)
            cum = jnp.cumsum(sp, axis=-1)
            exceed = cum > top_p
            first_idx = jnp.argmax(exceed, axis=-1)
            first = jnp.arange(probs.shape[-1])[None, :] == first_idx[:, None]
            keep = ~exceed | first
            kept = jnp.where(keep, sp, 0.0)
            t_idx = jnp.arange(probs.shape[0])[:, None]
            return jnp.zeros_like(probs).at[t_idx, order].set(kept)
        s, b, h = hidden_states.shape
        x = hidden_states.reshape(-1, h)
        probs = jax.nn.softmax(x @ router_w.T, axis=-1)
        w = _top_p_weights(probs, TOP_P)
        out = jnp.zeros_like(x)
        n_exp = router_w.shape[0]
        for e in range(n_exp):
            g = jax.nn.silu(x @ gate_w[e].T)
            u = x @ up_w[e].T
            y = g * u @ down_w[e].T
            out = out + y * w[:, e:e + 1]
        return out.reshape(s, b, h)
    x = L0_attn_x
    x = x + _layernorm(_L0_attn_ref(_layernorm(x, axis=-1), L0_attn_Wq, L0_attn_bq, L0_attn_Bq, L0_attn_Aq, L0_attn_Wk, L0_attn_bk, L0_attn_Bk, L0_attn_Ak, L0_attn_Wv, L0_attn_bv, L0_attn_Bv, L0_attn_Av, L0_attn_Wo, L0_attn_bo, L0_attn_Bo, L0_attn_Ao), axis=-1)
    x = x + _layernorm(_L0_ffn_ref(_layernorm(x, axis=-1), L0_ffn_Wg, L0_ffn_bg, L0_ffn_Wup, L0_ffn_bup, L0_ffn_Wsw, L0_ffn_bsw, L0_ffn_Wdn, L0_ffn_bdn, L0_ffn_Wsu, L0_ffn_bsu, L0_ffn_Wsa, L0_ffn_bsa, L0_ffn_Wsd, L0_ffn_bsd), axis=-1)
    x = x + _layernorm(_L1_attn_ref(_layernorm(x, axis=-1), L1_attn_Wq, L1_attn_Wk, L1_attn_Wv, L1_attn_Wo), axis=-1)
    x = x + _layernorm(_L1_ffn_ref(_layernorm(x, axis=-1), L1_ffn_router_w, L1_ffn_gate_w, L1_ffn_up_w, L1_ffn_down_w), axis=-1)
    return x

_drawn_inputs = setup_inputs


def setup_inputs(seed=0):
    import zlib

    import numpy as np

    out = dict(_drawn_inputs(seed))
    spreads = {'L0_ffn_bg': (0.0, 0.8),
     'L0_ffn_bup': (0.0, 0.8),
     'L0_ffn_bsw': (0.0, 0.8),
     'L0_ffn_bdn': (0.0, 0.423),
     'L0_ffn_bsu': (0.0, 0.8),
     'L0_ffn_bsa': (0.0, 0.8),
     'L0_ffn_bsd': (0.0, 0.445)}
    factors = {'L0_attn_bq': 8.0,
     'L0_attn_Bq': 8.0,
     'L0_attn_Aq': 8.0,
     'L0_attn_bk': 64.0,
     'L0_attn_Bk': 8.0,
     'L0_attn_Ak': 8.0,
     'L0_attn_Bv': 3.351,
     'L0_attn_Av': 5.275,
     'L0_ffn_Wg': 4.537,
     'L0_ffn_Wup': 8.0,
     'L0_ffn_Wsw': 8.0,
     'L0_ffn_Wdn': 8.0,
     'L0_ffn_Wsu': 8.0,
     'L0_ffn_Wsa': 8.0,
     'L0_ffn_Wsd': 8.0,
     'L1_attn_Wq': 8.0,
     'L1_attn_Wk': 8.0}
    for name, (base, spread) in spreads.items():
        noise = np.random.default_rng([zlib.crc32(name.encode()), seed]).standard_normal(out[name].shape)
        drawn = base * np.exp(spread * noise) if base else spread * noise
        out[name] = jnp.asarray(drawn.astype(out[name].dtype))
    for name, factor in factors.items():
        out[name] = (out[name] * factor).astype(out[name].dtype)
    return out
```

```python
from contextlib import ExitStack

import numpy as np

import concourse.bass as bass
from concourse import mybir

F32 = mybir.dt.float32
F32R = mybir.dt.float32r
BF16 = mybir.dt.bfloat16
ALU = mybir.AluOpType
ACT = mybir.ActivationFunctionType
AX = mybir.AxisListType

P = 128
T = 1024
NT = T // P
HALF = 512
D = 256
NC = D // P
HEADS, HD = 16, 16
GROUPS, GH = 4, 4
PARTS = 3
Q_SLOT = [0, 0, 0, 1, 1, 2]
K_SLOT = [0, 1, 2, 0, 1, 0]
SLOTS = len(Q_SLOT)
KS = SLOTS * HD
KM = KS + PARTS
VW = HD + 1
BIG = -3.0e38
EPS = 1e-5
N0 = 8
E0 = 6
ROUNDS = 2
E1 = 8
I1 = 512 // P
TOP_P = 0.9
ARENA = 212480
UPTO = 4
LEAD = 12


def program(nc, a, out):
    ctx = ExitStack()
    with ctx:
        ctx.enter_context(nc.sbuf_tensor("arena", [P, ARENA], mybir.dt.uint8))
        build(nc, a, out, ctx)


def build(nc, a, out, ctx):
    K = 1024
    base = nc.sbuf_base - ARENA

    def sb(name, shape, dt, at):
        size = int(np.prod(shape[1:])) * (2 if dt == BF16 else 4)
        assert at % 32 == 0 and at + size <= ARENA, (name, at, size)
        return nc.alloc_sbuf_tensor_at(name, shape, dt, offset=base + at)

    A_, C_, D_, E_, F_, G_, H_, I_, J_ = (0, 24 * K, 56 * K, 80 * K, 96 * K, 105 * K, 129 * K, 177 * K, 189 * K)
    x_res = sb("x_res", [P, NT, D], F32, A_)
    xhi = sb("xhi", [P, NC, T], F32R, A_ + 8 * K)
    xlo = sb("xlo", [P, NC, T], F32R, A_ + 16 * K)
    qa = [sb(f"qa{i}", [P, 2, GH, HALF], BF16, C_ + 8 * K * i) for i in range(2)]
    ka = [sb(f"ka{i}", [P, GH, T], BF16, C_ + 16 * K + 8 * K * i) for i in range(2)]
    parts = [sb(f"parts{i}", [P, PARTS, T], BF16, D_ + 6 * K * i) for i in range(4)]
    qf = sb("qf", [P, 2, HALF], F32, E_)
    qd = sb("qd", [P, 2, HALF], F32, E_ + 4 * K)
    rot = sb("rot", [P, 2, 2, HALF], F32, E_ + 8 * K)
    o_t = sb("o_t", [P, 2, HALF], F32, E_)
    attn = sb("attn", [P, NT, D], F32, E_ + 4 * K)
    vaug = sb("vaug", [P, NT, 288], F32, F_)
    pt = sb("pt", [P, 6, 2, HALF], F32, G_)
    wqkv_hi = sb("wqkv_hi", [P, 3, NC, D], F32R, G_)
    wqkv_lo = sb("wqkv_lo", [P, 3, NC, D], F32R, G_ + 6 * K)
    wraw = sb("wraw", [P, 4, NC, D], F32, H_)
    weff = sb("weff", [P, 4, NC, D], F32, H_ + 8 * K)
    lora = sb("lora", [16, 2, 4, D], F32, H_ + 16 * K)
    stage = sb("stage", [P, 3072], F32, I_)
    jo = [J_]

    def small(name, shape, dt):
        t = sb(name, shape, dt, jo[0])
        jo[0] += -(-int(np.prod(shape[1:])) * (2 if dt == BF16 else 4) // 32) * 32
        return t

    ident = small("ident", [P, P], F32)
    ident_b = small("ident_b", [P, P], BF16)
    wo_hi = small("wo_hi", [P, NC, D], F32R)
    wo_lo = small("wo_lo", [P, NC, D], F32R)
    mask_raw = small("mask_raw", [P, 2, P], F32)
    mask_b = small("mask_b", [P, 2, P], BF16)
    tri = small("tri", [P, 8, 8], F32)
    bqk = small("bqk", [P, 2, NC], F32)
    bv_b = small("bv_b", [P, D], F32)
    bo_b = small("bo_b", [P, D], F32)
    mhalf = small("mhalf", [P, NT], F32)
    stats = small("stats", [P, NT, 6], F32)
    mv = small("mv", [P, NT, 2], F32)
    rstd = small("rstd", [P, NT], F32)
    mx = small("mx", [P, 2, 16, 2], F32)
    nmf = small("nmf", [P, 2, 16], F32)
    nmd = small("nmd", [P, 2, 16], F32)
    nmp = small("nmp", [P, 2, PARTS, 16], BF16)
    nmt = small("nmt", [48, 2, P], BF16)
    rden = small("rden", [P, 2, 4, GH], F32)
    sel = small("sel", [96, 8, P], F32R)
    bst = small("bst", [96, D], F32R)
    bst_raw = small("bst_raw", [96, D], F32)
    b_up = small("b_up", [P, N0], F32)
    b_sw = small("b_sw", [P, N0], F32)
    b_sd = small("b_sd", [P, NC], F32)
    bg_b = small("bg_b", [P, ROUNDS, 8], F32)
    sel_raw = sb("sel_raw", [96, 8, P], F32, H_ + 28 * K)
    w_up_hi, w_up_lo = (sb(f"w_up_{i}", [P, N0, NC, P], F32R, H_ + 20 * K * j) for j, i in enumerate(("hi", "lo")))
    w_sw_hi, w_sw_lo = (sb(f"w_sw_{i}", [P, N0, P], F32R, H_ + 8 * K + 20 * K * j) for j, i in enumerate(("hi", "lo")))
    w_dn_hi, w_dn_lo = (sb(f"w_dn_{i}", [P, N0, D], F32R, H_ + 12 * K + 20 * K * j) for j, i in enumerate(("hi", "lo")))
    wg_sb = small("wg_sb", [P, ROUNDS, NC, 8], F32)
    res_t = sb("res_t", [P, NC, T], F32, C_)
    xc_t = sb("xc_t", [P, NC, T], F32, C_ + 8 * K)
    wb0 = sb("wb0", [P, 2, E0, HALF], F32, C_ + 16 * K)
    wt0 = sb("wt0", [96, 2, HALF], F32R, 64 * K)
    wst = sb("wst", [P, 4, 96], F32R, 68 * K)
    f_s = sb("f_s", [P, 2, HALF], F32, 70 * K)
    f_sw = sb("f_sw", [P, 2, HALF], F32, 74 * K)
    f_g = sb("f_g", [P, 2, HALF], F32, 78 * K)
    h_hi = sb("h_hi", [P, 2, HALF], F32R, 82 * K)
    h_lo = sb("h_lo", [P, 2, HALF], F32R, 86 * K)
    g_hi = sb("g_hi", [P, 3, HALF], F32R, 90 * K)
    g_lo = sb("g_lo", [P, 3, HALF], F32R, 96 * K)
    gate_at = 102 * K
    gl, g_e, g_w = (sb(n, [P, 4, 8], F32, gate_at + 128 * i) for i, n in enumerate(("gl", "g_e", "g_w")))
    g_m, g_r = (sb(n, [P, 4], F32, gate_at + 384 + 32 * i) for i, n in enumerate(("g_m", "g_r")))
    g_rank = sb("g_rank", [P, 4, 8], F32, gate_at + 448)
    g_gt = sb("g_gt", [P, 4, 8, 8], F32, gate_at + 1024)
    g_eq = sb("g_eq", [P, 4, 8, 8], F32, gate_at + 2048)
    g_base = sb("g_base", [P, 4, 8], F32, gate_at + 704)
    w1q_hi, w1q_lo = (sb(f"w1q_{i}", [P, 2, NC, D], F32R, G_ + 6784 * j) for j, i in enumerate(("hi", "lo")))
    w1k_hi, w1k_lo = (sb(f"w1k_{i}", [P, 2, NC, P], F32R, G_ + 4096 + 6784 * j) for j, i in enumerate(("hi", "lo")))
    w1v_hi, w1v_lo = (sb(f"w1v_{i}", [P, NC, 64], F32R, G_ + 6144 + 6784 * j) for j, i in enumerate(("hi", "lo")))
    rope = sb("rope", [P, 2, T], F32, G_ + 14 * K)
    w1 = [[sb(f"w1_{n}{b}", [P, 3, 1024], F32R, H_ + 24 * K * b + 12 * K * j) for j, n in enumerate(("hi", "lo"))]
          for b in range(2)]
    raw1 = [stage, sb("stage2", [P, 3072], F32, D_)]
    wb1 = sb("wb1", [P, E1, T], F32, C_)
    x1_t = sb("x1_t", [P, NC, T], F32, 68 * K)
    wt1 = sb("wt1", [96, T], F32R, 76 * K)
    wst1 = sb("wst1", [P, NT, 96], F32R, 80 * K)
    y1_t = sb("y1_t", [P, NC, T], F32, 68 * K)
    m_s = sb("m_s", [P, 3, HALF], F32, 84 * K)
    m_sw = sb("m_sw", [P, 3, HALF], F32, 90 * K)
    m_g = sb("m_g", [P, 2, HALF], F32, 96 * K)
    m_ghi = sb("m_ghi", [P, 3, HALF], F32R, 100 * K)
    m_glo = sb("m_glo", [P, 3, HALF], F32R, 106 * K)
    r_at = 112 * K
    r_l, r_e, r_p, r_x, r_w = (sb(n, [P, NT, 8], F32, r_at + 256 * i)
                               for i, n in enumerate(("r_l", "r_e", "r_p", "r_x", "r_w")))
    r_m, r_s = (sb(n, [P, NT], F32, r_at + 1280 + 32 * i) for i, n in enumerate(("r_m", "r_s")))
    r_gt = sb("r_gt", [P, NT, 8, 8], F32, r_at + 2 * K)
    r_eq = sb("r_eq", [P, NT, 8, 8], F32, r_at + 4 * K)
    rw_sb = sb("rw_sb", [P, NC, 8], F32, r_at + 6 * K)
    PS = ctx.enter_context(nc.psum_tensor("PS", [P, 8, HALF], F32))

    sems = {}

    def sem(name):
        assert name not in sems, name
        sems[name] = ctx.enter_context(nc.semaphore(name))
        return sems[name]

    class Stage:

        @staticmethod
        def sync(sp):
            pass

        @staticmethod
        def gpsimd(pool):
            pass

        @staticmethod
        def scalar(act):
            pass

        @staticmethod
        def vector(dve):
            pass

        @staticmethod
        def tensor(pe):
            pass

    stages = []
    scr_q = nc.dram_tensor("scr_q", [2, PARTS, P, T], BF16).ap()
    scr_k = nc.dram_tensor("scr_k", [2, PARTS, P, T], BF16).ap()

    s_x = sem("x_loaded")
    s_cst = sem("consts_loaded")
    s_w0 = sem("attn0_weights_loaded")
    s_cst_b = sem("consts_ready")
    CONSTS, LOADED = 7, 16 * 12

    class Start(Stage):
        @staticmethod
        def sync(sp):
            for hf in range(2):
                sp.dma_start(x_res[:, 4 * hf:4 * hf + 4, :],
                             a["x"].rearrange("(t p) d -> p t d", p=P)[:, 4 * hf:4 * hf + 4, :]).then_inc(s_x, 16)
            sp.dma_start(lora[:], a["lora"].rearrange("k m r o -> r k m o")).then_inc(s_w0, 16)
            sp.dma_start(wraw[:], a["w_attn0"].rearrange("m (c p) o -> p m c o", p=P)).then_inc(s_w0, 16)

        @staticmethod
        def scalar(act):
            act.dma_start(ident[:], a["ident"]).then_inc(s_cst, 16)
            act.dma_start(bqk[:], a["bqk"]).then_inc(s_cst, 16)
            act.dma_start(bv_b[:], a["bvo"][0:1, :].broadcast_to([P, D])).then_inc(s_cst, 16)
            act.dma_start(bo_b[:], a["bvo"][1:2, :].broadcast_to([P, D])).then_inc(s_cst, 16)
            act.dma_start(mask_raw[:], a["masks"]).then_inc(s_cst, 16)
            act.dma_start(tri[:], a["tri"]).then_inc(s_cst, 16)
            act.dma_start(sel_raw[:], a["sel"]).then_inc(s_cst, 16)
            act.dma_start(bst_raw[:], a["b_dn0"]).then_inc(s_cst, 16)
            act.dma_start(b_up[:], a["b_up0"]).then_inc(s_cst, 16)
            act.dma_start(b_sw[:], a["b_sw0"]).then_inc(s_cst, 16)
            act.dma_start(b_sd[:], a["b_sd0"]).then_inc(s_cst, 16)
            act.dma_start(bg_b[:], a["b_g0"].broadcast_to([P, ROUNDS, 8])).then_inc(s_cst, 16)

        @staticmethod
        def gpsimd(pool):
            pool.memset(mhalf[:], -0.5).then_inc(s_cst_b, 1)
            pool.wait_ge(s_cst_b, 1)
            pool.memset(vaug[:], 1.0).then_inc(s_cst_b, 1)
            pool.wait_ge(s_cst_b, 2)
            pool.memset(ka[0][96:99, :, :], 1.0).then_inc(s_cst_b, 1)
            pool.wait_ge(s_cst_b, 3)
            pool.memset(ka[1][96:99, :, :], 1.0).then_inc(s_cst_b, 1)
            pool.wait_ge(s_cst, LOADED)
            pool.wait_ge(s_cst_b, 4)
            pool.tensor_copy(ident_b[:], ident[:]).then_inc(s_cst_b, 1)
            pool.wait_ge(s_cst_b, 5)
            pool.tensor_copy(mask_b[:], mask_raw[:]).then_inc(s_cst_b, 1)
            pool.wait_ge(s_cst_b, 6)
            pool.tensor_copy(sel[:], sel_raw[:]).then_inc(s_cst_b, 1)

    stages.append(Start)

    class Norm:
        stat = sem("norm_stats")
        var = sem("norm_var")
        rstd = sem("norm_rstd")
        y = sem("norm_done")
        norms = 0

        def __init__(self):
            self.stat0, self.half0, self.y0 = 2 * NT * Norm.norms, 2 * Norm.norms, NT * Norm.norms
            Norm.norms += 1

        def moments(self, dve, hf, src, before=None, free=None):
            for i in range(4):
                t = 4 * hf + i
                if before:
                    before(dve, t)
                dve.bn_stats(stats[:, t, :], src(t)).then_inc(self.stat, 1)
            dve.wait_ge(self.stat, self.stat0 + 8 * hf + 4)
            for i in range(4):
                t = 4 * hf + i
                dve.bn_aggr(mv[:, t, :], stats[:, t, :]).then_inc(self.stat, 1)

        def power(self, pool, hf):
            ts = slice(4 * hf, 4 * hf + 4)
            pool.wait_ge(self.stat, self.stat0 + 8 * hf + 8)
            pool.wait_ge(s_cst_b, 1)
            pool.tensor_scalar(rstd[:, ts], mv[:, ts, 1], EPS, None, ALU.add).then_inc(self.var, 1)
            pool.wait_ge(self.var, self.half0 + hf + 1)
            pool.tensor_tensor(rstd[:, ts], rstd[:, ts], mhalf[:, ts], ALU.pow).then_inc(self.rstd, 1)

        def apply(self, dve, hf, src, dst):
            dve.wait_ge(self.rstd, self.half0 + hf + 1)
            for i in range(4):
                t = 4 * hf + i
                dve.tensor_scalar(dst(t), src(t), mv[:, t, 0:1], rstd[:, t:t + 1], ALU.subtract, ALU.mult)\
                   .then_inc(self.y, 1)

    def pre_norm(tag, xn, wait_x, keep=()):
        n = Norm()
        s_t = sem(tag + "_transposed")
        s_hi = sem(tag + "_hi")
        s_lo = sem(tag + "_lo")
        s_keep = sem(tag + "_kept")

        class Pre(Stage):
            norm, hi, lo, kept = n, s_hi, s_lo, s_keep

            @staticmethod
            def vector(dve):
                for hf in range(2):
                    wait_x(dve, hf)
                    n.moments(dve, hf, lambda t: x_res[:, t, :])
                    n.apply(dve, hf, lambda t: x_res[:, t, :], lambda t: xn[:, t, :])
                for hf in range(2):
                    for c in range(NC):
                        k = 2 * hf + c
                        dve.wait_ge(s_hi, k + 1)
                        if keep:
                            dve.wait_ge(s_keep, k + 1)
                        dve.tensor_tensor(xlo[:, c, HALF * hf:HALF * hf + HALF], PS[:, k, :],
                                          xhi[:, c, HALF * hf:HALF * hf + HALF].bitcast(F32), ALU.subtract)\
                           .then_inc(s_lo, 1)

            @staticmethod
            def gpsimd(pool):
                for hf in range(2):
                    n.power(pool, hf)

            @staticmethod
            def tensor(pe):
                pe.wait_ge(s_cst_b, CONSTS)
                for hf in range(2):
                    pe.wait_ge(n.y, n.y0 + 4 * hf + 4)
                    for c in range(NC):
                        for i in range(4):
                            m = pe.transpose(PS[:, 2 * hf + c, P * i:P * i + P],
                                             xn[:, 4 * hf + i, P * c:P * c + P], ident[:])
                        m.then_inc(s_t, 1)

            @staticmethod
            def scalar(act):
                for hf in range(2):
                    for c in range(NC):
                        k = 2 * hf + c
                        act.wait_ge(s_t, k + 1)
                        act.activation(xhi[:, c, HALF * hf:HALF * hf + HALF], PS[:, k, :], ACT.Copy)\
                           .then_inc(s_hi, 1)
                        for dst in keep:
                            act.activation(dst[:, c, HALF * hf:HALF * hf + HALF], PS[:, k, :], ACT.Copy)\
                               .then_inc(s_keep, 1)
        return Pre

    def post_norm(tag, src, wait_src, y):
        n = Norm()
        s_new = sem(tag + "_x")

        class Post(Stage):
            x = s_new

            @staticmethod
            def vector(dve):
                for hf in range(2):
                    wait_src(dve, hf)
                    n.moments(dve, hf, src)
                    n.apply(dve, hf, src, lambda t: y[:, t, :])
                    for i in range(4):
                        t = 4 * hf + i
                        dve.wait_ge(n.y, n.y0 + t + 1)
                        dve.tensor_tensor(x_res[:, t, :], x_res[:, t, :], y[:, t, :], ALU.add).then_inc(s_new, 1)

            @staticmethod
            def gpsimd(pool):
                for hf in range(2):
                    n.power(pool, hf)
        return Post

    xn = sb("xn", [P, NT, D], F32, G_ + 12 * K)
    pre0 = pre_norm("pre0", xn, lambda dve, hf: dve.wait_ge(s_x, 32))
    s_lora = sem("lora_product")
    s_weff = sem("w_eff")
    s_whi = sem("w_eff_hi")
    s_wlo = sem("w_eff_lo")

    def w0(m, lo):
        if m == 3:
            return wo_lo if lo else wo_hi
        return (wqkv_lo if lo else wqkv_hi)[:, m, :, :]

    class Weights0(Stage):

        @staticmethod
        def tensor(pe):
            pe.wait_ge(s_w0, 32)
            for m in range(4):
                for c in range(NC):
                    mm = pe.matmul(PS[:, 4 + m, D * c:D * c + D], lora[:, 1, m, P * c:P * c + P], lora[:, 0, m, :],
                                   start=True, stop=True)
                mm.then_inc(s_lora, 1)

        @staticmethod
        def vector(dve):
            dve.wait_ge(s_w0, 32)
            for m in range(4):
                dve.wait_ge(s_lora, m + 1)
                dve.scalar_tensor_tensor(weff[:, m, :, :], PS[:, 4 + m, :].rearrange("p (c o) -> p c o", c=NC), 0.5,
                                         wraw[:, m, :, :], ALU.mult, ALU.add).then_inc(s_weff, 1)
            for m in range(4):
                dve.wait_ge(s_whi, m + 1)
                dve.tensor_tensor(w0(m, 1)[:], weff[:, m, :, :], w0(m, 0)[:].bitcast(F32), ALU.subtract)\
                   .then_inc(s_wlo, 1)

        @staticmethod
        def scalar(act):
            for m in range(4):
                act.wait_ge(s_weff, m + 1)
                act.activation(w0(m, 0)[:], weff[:, m, :, :], ACT.Copy).then_inc(s_whi, 1)

    stages.append(Weights0)
    stages.append(pre0)

    def product(pe, ps, w_hi, w_lo, x_hi, x_lo, chunks, start=True, stop=True):
        n = 3 * chunks
        k = 0
        for c in range(chunks):
            for w, x in ((w_hi, x_hi), (w_lo, x_hi), (w_hi, x_lo)):
                m = pe.matmul(ps, w(c), x(c), start=start and k == 0, stop=stop and k == n - 1)
                k += 1
        return m

    def split_parts(tag, units):
        s_f = sem(tag + "_f32")
        s_p1, s_d, s_p2, s_p3 = (sem(tag + x) for x in ("_part1", "_rest", "_part2", "_part3"))

        class Split:
            f, p1, d, p2, p3 = s_f, s_p1, s_d, s_p2, s_p3

            @staticmethod
            def free(eng, n):
                if n >= 2:
                    eng.wait_ge(s_p1, n - 1)
                    eng.wait_ge(s_d, n - 1)

            @staticmethod
            def act_first(act, n):
                dst, hf = units[n]
                act.wait_ge(s_f, n + 1)
                act.activation(dst[:, 0, HALF * hf:HALF * hf + HALF], qf[:, n % 2, :], ACT.Copy).then_inc(s_p1, 1)

            @staticmethod
            def act_second(act, n):
                dst, hf = units[n]
                act.wait_ge(s_d, n + 1)
                act.activation(dst[:, 1, HALF * hf:HALF * hf + HALF], qd[:, n % 2, :], ACT.Copy).then_inc(s_p2, 1)

            @staticmethod
            def dve_first(dve, n):
                dst, hf = units[n]
                dve.wait_ge(s_p1, n + 1)
                if n >= 2:
                    dve.wait_ge(s_p2, n - 1)
                    dve.wait_ge(s_p3, n - 1)
                dve.tensor_tensor(qd[:, n % 2, :], qf[:, n % 2, :], dst[:, 0, HALF * hf:HALF * hf + HALF],
                                  ALU.subtract).then_inc(s_d, 1)

            @staticmethod
            def dve_second(dve, n):
                dst, hf = units[n]
                dve.wait_ge(s_p2, n + 1)
                dve.wait_ge(s_d, n + 1)
                dve.tensor_tensor(dst[:, 2, HALF * hf:HALF * hf + HALF], qd[:, n % 2, :],
                                  dst[:, 1, HALF * hf:HALF * hf + HALF], ALU.subtract).then_inc(s_p3, 1)
        return Split

    units0 = [(op, m, hf) for m in range(2) for op in range(2) for hf in range(2)]
    split0 = split_parts("qk0", [(parts[2 * m + op], hf) for op, m, hf in units0])
    s_qk0 = sem("qk0_product")
    s_v0 = sem("v0_product")
    s_vaug0 = sem("v0_ready")
    s_scr0 = [sem(f"qk0_in_scratch{m}") for m in range(2)]

    class Project0(Stage):
        @staticmethod
        def tensor(pe):
            pe.wait_ge(s_wlo, 3)
            for n, (op, m, hf) in enumerate(units0):
                pe.wait_ge(pre0.lo, 2 * hf + 2)
                if n >= 2:
                    pe.wait_ge(split0.f, n - 1)
                h = slice(HALF * hf, HALF * hf + HALF)
                product(pe, PS[:, 4 + n % 2, :],
                        lambda c: wqkv_hi[:, op, c, P * m:P * m + P], lambda c: wqkv_lo[:, op, c, P * m:P * m + P],
                        lambda c: xhi[:, c, h], lambda c: xlo[:, c, h], NC).then_inc(s_qk0, 1)
            for n in range(NT):
                t = slice(P * n, P * n + P)
                if n >= 4:
                    pe.wait_ge(s_vaug0, n - 3)
                product(pe, PS[:, (6, 7, 2, 3)[n % 4], 0:D], lambda c: xhi[:, c, t], lambda c: xlo[:, c, t],
                        lambda c: wqkv_hi[:, 2, c, :], lambda c: wqkv_lo[:, 2, c, :], NC).then_inc(s_v0, 1)

        @staticmethod
        def scalar(act):
            act.wait_ge(s_cst, LOADED)
            for n, (op, m, hf) in enumerate(units0):
                act.wait_ge(s_qk0, n + 1)
                split0.free(act, n)
                act.activation(qf[:, n % 2, :], PS[:, 4 + n % 2, :], ACT.Identity, bias=bqk[:, op, m:m + 1])\
                   .then_inc(split0.f, 1)
                split0.act_first(act, n)
                if n >= 1:
                    split0.act_second(act, n - 1)
            split0.act_second(act, len(units0) - 1)

        @staticmethod
        def vector(dve):
            for n in range(len(units0)):
                split0.dve_first(dve, n)
                if n >= 1:
                    split0.dve_second(dve, n - 1)
            split0.dve_second(dve, len(units0) - 1)
            dve.wait_ge(s_cst_b, CONSTS)
            for n in range(NT):
                dve.wait_ge(s_v0, n + 1)
                dve.tensor_tensor(vaug[:, n, 0:HEADS * VW].rearrange("p (h w) -> p h w", w=VW)[:, :, 0:HD],
                                  PS[:, (6, 7, 2, 3)[n % 4], 0:D].rearrange("p (h w) -> p h w", w=HD),
                                  bv_b[:].rearrange("p (h w) -> p h w", w=HD), ALU.add).then_inc(s_vaug0, 1)

        @staticmethod
        def sync(sp):
            for m in range(2):
                for op, scr in enumerate((scr_q, scr_k)):
                    n = 4 * m + 2 * op + 2
                    sp.wait_ge(split0.p3, n)
                    sp.dma_start(scr[m].rearrange("s p t -> p s t"), parts[2 * m + op][:]).then_inc(s_scr0[m], 16)

    stages.append(Project0)

    def attention(tag, causal, s_scr, scr_count, v_ready, kv_heads, extra_pool=None):
        units = [(g, qh) for g in range(GROUPS) for qh in range(2)]
        steps, tstart = [], []
        for u, (g, qh) in enumerate(units):
            tstart.append(len(steps))
            for kt in range(4 * (qh + 1) if causal else NT):
                steps.append((u, kt, max(0, P * kt - HALF * qh) if causal else 0))
        tstart.append(len(steps))
        NS = len(steps)
        tiles, send = [], []
        for u, (g, qh) in enumerate(units):
            for hl in range(GH):
                for qt in range(4):
                    keys = P * (4 * qh + qt + 1) if causal else T
                    for kh in range(-(-keys // HALF)):
                        tiles.append((u, hl, qt, kh, min(HALF, keys - HALF * kh)))
            send.append(len(tiles))
        assert len(tiles) == 4 * NS
        n_kh = [1 if causal and qh == 0 else 2 for g, qh in units]
        s_s = sem(tag + "_scores")
        s_max = sem(tag + "_tile_max")
        s_nm = sem(tag + "_negated_max")
        NM = 4
        s_neg = sem(tag + "_unit_max")
        s_nmT = sem(tag + "_max_transposed")
        s_nmE = sem(tag + "_max_evacuated")
        s_nmR = [sem(f"{tag}_max_rows{i}") for i in range(2)]
        s_T = sem(tag + "_scoresT")
        s_e = sem(tag + "_exp")
        s_pv = sem(tag + "_pv")
        s_oE = sem(tag + "_out_evacuated")
        s_oT = sem(tag + "_out_transposed")
        s_rd = sem(tag + "_reciprocal")
        s_at = sem(tag + "_attn")
        s_ld = [sem(f"{tag}_operands{i}") for i in range(2)]
        k_once = kv_heads == GROUPS
        per_q, per_k = 2 * SLOTS * 16, SLOTS * 16

        def operands(eng, g):
            eng.wait_ge(s_ld[g % 2], (g // 2 + 1) * (per_q + (0 if k_once else per_k)) + (per_k if k_once else 0)
                        if (not k_once or g % 2 == 0) else (g // 2 + 1) * per_q)
            if k_once and g % 2 == 1:
                eng.wait_ge(s_ld[0], per_q + per_k)

        def load(sp, g):
            m, off = g // 2, 64 * (g % 2)
            for i in range(SLOTS):
                for qh in range(2):
                    sp.dma_start(qa[g % 2][HD * i:HD * i + HD, qh, :, :],
                                 scr_q[m, Q_SLOT[i], off:off + 64, HALF * qh:HALF * qh + HALF]
                                 .rearrange("(h d) t -> d h t", h=GH)).then_inc(s_ld[g % 2], 16)
            if not k_once or g == 0:
                for i in range(SLOTS):
                    sp.dma_start(ka[g % 2][HD * i:HD * i + HD, :, :],
                                 scr_k[m, K_SLOT[i], off:off + 64, :].rearrange("(h d) t -> d h t", h=GH))\
                      .then_inc(s_ld[g % 2], 16)

        def kop(g, hl):
            return (ka[0], g) if k_once else (ka[g % 2], hl)

        def tiles_before(s):
            return min(len(tiles), 4 * (s + LEAD))

        class Att(Stage):
            attn_ready = s_at
            pv = s_pv
            n_steps = NS

            @staticmethod
            def sync(sp):
                def scratch(m):
                    sp.wait_ge(s_scr[m], scr_count[m])
                scratch(0)
                load(sp, 0)
                load(sp, 1)
                for v in range(len(units)):
                    g, qh = units[v]
                    sp.wait_ge(s_nmE, v + 1)
                    for p in range(PARTS):
                        sp.dma_start(qa[g % 2][KS + p:KS + p + 1, qh, :, :].rearrange("p h c -> p (h c)")
                                     .rearrange("p (r c) -> p r c", c=P),
                                     nmt[16 * p:16 * p + 16, v % 2, :]).then_inc(s_nmR[v % 2], 16)
                    if qh == 0 and 1 <= g <= 2:
                        scratch(1)
                        sp.wait_ge(s_T, 2 * tstart[2 * g])
                        load(sp, g + 1)

            @staticmethod
            def gpsimd(pool):
                for v in range(len(units)):
                    b = v % 2
                    pool.wait_ge(s_neg, v + 1)
                    if v >= 2:
                        pool.wait_ge(s_nmT, v - 1)
                    k = NM * v
                    pool.tensor_copy(nmp[:, b, 0, :], nmd[:, b, :]).then_inc(s_nm, 1)
                    pool.wait_ge(s_nm, k + 1)
                    pool.tensor_tensor(nmf[:, b, :], nmd[:, b, :], nmp[:, b, 0, :], ALU.subtract).then_inc(s_nm, 1)
                    pool.wait_ge(s_nm, k + 2)
                    pool.tensor_copy(nmp[:, b, 1, :], nmf[:, b, :]).then_inc(s_nm, 1)
                    pool.wait_ge(s_nm, k + 3)
                    pool.tensor_tensor(nmp[:, b, 2, :], nmf[:, b, :], nmp[:, b, 1, :], ALU.subtract).then_inc(s_nm, 1)
                    if extra_pool:
                        extra_pool(pool, v)

            @staticmethod
            def tensor(pe):
                misc = [None]

                def misc_free():
                    if misc[0]:
                        pe.wait_ge(*misc[0])

                def s_tile(i):
                    u, hl, qt, kh, w = tiles[i]
                    g, qh = units[u]
                    if i == 0 or units[tiles[i - 1][0]][0] != g:
                        operands(pe, g)
                    if i >= 2:
                        pe.wait_ge(s_max, i - 1)
                    kb, kx = kop(g, hl)
                    diag = causal and HALF * kh + w == P * (4 * qh + qt + 1)
                    m = pe.matmul(PS[:, i % 2, 0:w], qa[g % 2][0:KS, qh, hl, P * qt:P * qt + P],
                                  kb[0:KS, kx, HALF * kh:HALF * kh + w], start=True, stop=not diag)
                    if diag:
                        m = pe.matmul(PS[:, i % 2, w - P:w], ident_b[:], mask_b[:, 0, :], start=False, stop=True)
                    m.then_inc(s_s, 1)

                def max_rows(v):
                    misc_free()
                    pe.wait_ge(s_nm, NM * v + NM)
                    pe.transpose(PS[0:48, 7, 0:64].bitcast(BF16), nmp[:, v % 2, :, :].rearrange("p s r -> p (s r)"),
                                 ident_b[:]).then_inc(s_nmT, 1)
                    misc[0] = (s_nmE, v + 1)

                def out_tiles(v):
                    misc_free()
                    pe.wait_ge(s_oE, v + 1)
                    for i in range(4):
                        m = pe.transpose(PS[:, 7, P * i:P * i + P], o_t[:, v % 2, P * i:P * i + P], ident[:])
                    m.then_inc(s_oT, 1)
                    misc[0] = (s_at, v + 1)

                def pv(s):
                    u, kt, q0 = steps[s]
                    g, qh = units[u]
                    pe.wait_ge(s_e, 2 * s + 2)
                    if kt == 0 and u >= 1:
                        pe.wait_ge(s_oE, u)
                    last = s == tstart[u + 1] - 1
                    for hl in range(GH):
                        w = VW * (g if k_once else GH * g + hl)
                        m = pe.matmul(PS[32 * hl:32 * hl + 32, 6, q0:HALF], vaug[:, kt, w:w + 32],
                                      pt[:, (2 * s + hl // 2) % 6, hl % 2, q0:HALF], start=kt == 0, stop=last)
                    m.then_inc(s_pv, 1)

                first = send[0]
                for i in range(first):
                    s_tile(i)
                v_ready(pe)
                done = first
                max_rows(0)
                for s in range(NS + 4):
                    for v in range(len(units)):
                        if v >= 1 and s == max(1, tstart[v] - 3):
                            while done < send[v]:
                                s_tile(done)
                                done += 1
                            max_rows(v)
                        if s == tstart[v + 1] + 2:
                            out_tiles(v)
                    if s < NS:
                        u, kt, q0 = steps[s]
                        g, qh = units[u]
                        if s == tstart[u]:
                            pe.wait_ge(s_nmR[u % 2], 48 * (u // 2 + 1))
                        for pr in range(2):
                            pair = 2 * s + pr
                            if pair >= 2:
                                pe.wait_ge(s_e, pair - 1)
                            for hl in (2 * pr, 2 * pr + 1):
                                kb, kx = kop(g, hl)
                                diag = causal and P * kt >= HALF * qh
                                m = pe.matmul(PS[:, 2 + hl, q0:HALF], kb[0:KM, kx, P * kt:P * kt + P],
                                              qa[g % 2][0:KM, qh, hl, q0:HALF], start=True, stop=not diag)
                                if diag:
                                    m = pe.matmul(PS[:, 2 + hl, q0:q0 + P], ident_b[:], mask_b[:, 1, :],
                                                  start=False, stop=True)
                            m.then_inc(s_T, 1)
                            for _ in range(1):
                                if done < tiles_before(s + 1):
                                    s_tile(done)
                                    done += 1
                    if 1 <= s <= NS:
                        pv(s - 1)
                    if s < NS:
                        while done < tiles_before(s + 1):
                            s_tile(done)
                            done += 1
                    assert s < NS or done == len(tiles)

            @staticmethod
            def scalar(act):
                def max_evac(v):
                    act.wait_ge(s_nmT, v + 1)
                    if v >= 2:
                        act.wait_ge(s_nmR[v % 2], 48 * (v // 2))
                    act.activation(nmt[:, v % 2, :], PS[0:48, 7, 0:64].bitcast(BF16), ACT.Copy).then_inc(s_nmE, 1)

                max_evac(0)
                for s in range(NS + 1):
                    for v in range(1, len(units)):
                        if s == max(1, tstart[v] - 3):
                            max_evac(v)
                    if s < NS:
                        q0 = steps[s][2]
                        for pr in range(2):
                            pair = 2 * s + pr
                            act.wait_ge(s_T, pair + 1)
                            if pair >= 6:
                                act.wait_ge(s_pv, (pair - 6) // 2 + 1)
                            act.activation(pt[:, pair % 6, :, q0:HALF], PS[:, 2 + 2 * pr:4 + 2 * pr, q0:HALF],
                                           ACT.Exp, scale=0.25).then_inc(s_e, 1)
                    for v in range(len(units)):
                        if s == tstart[v + 1]:
                            act.wait_ge(s_pv, s)
                            if v >= 2:
                                act.wait_ge(s_oT, v - 1)
                            act.activation(o_t[:, v % 2, :], PS[:, 6, :], ACT.Copy).then_inc(s_oE, 1)

            @staticmethod
            def vector(dve):
                def normalise(v):
                    g, qh = units[v]
                    dve.wait_ge(s_oT, v + 1)
                    if v >= 2:
                        dve.wait_ge(s_at, v - 1)
                    o = PS[:, 7, :].rearrange("p (t h w) -> p t h w", t=4, w=32)
                    dve.reciprocal(rden[:, v % 2, :, :], o[:, :, :, HD]).then_inc(s_rd, 1)
                    dve.wait_ge(s_rd, v + 1)
                    dve.tensor_tensor(attn[:, 4 * qh:4 * qh + 4, GH * HD * g:GH * HD * (g + 1)]
                                      .rearrange("p t (h w) -> p t h w", w=HD), o[:, :, :, 0:HD],
                                      rden[:, v % 2, :, :].unsqueeze(3).broadcast_to([P, 4, GH, HD]), ALU.mult).then_inc(s_at, 1)

                todo = list(range(len(units)))
                for i in range(len(tiles)):
                    u, hl, qt, kh, w = tiles[i]
                    while todo and i >= tiles_before(tstart[todo[0] + 1] + 3) and tiles_before(tstart[todo[0] + 1] + 3) < len(tiles):
                        normalise(todo.pop(0))
                    dve.wait_ge(s_s, i + 1)
                    if hl == 0 and qt == 0 and kh == 0 and u >= 2:
                        dve.wait_ge(s_neg, u - 1)
                    dve.tensor_reduce(mx[:, u % 2, 4 * hl + qt, kh:kh + 1], PS[:, i % 2, 0:w], AX.X, ALU.max)\
                       .then_inc(s_max, 1)
                    if i + 1 == send[u]:
                        dve.wait_ge(s_max, i + 1)
                        if u >= 2:
                            dve.wait_ge(s_nm, NM * (u - 2) + 2)
                        dve.tensor_reduce(nmd[:, u % 2, :], mx[:, u % 2, :, 0:n_kh[u]], AX.X, ALU.max, negate=True)\
                           .then_inc(s_neg, 1)
                while todo:
                    normalise(todo.pop(0))
        return Att


    def out_projection(tag, att, wo_ready, bias):
        s_t = sem(tag + "_transposed")
        s_hi = sem(tag + "_hi")
        s_lo = sem(tag + "_lo")
        s_o = sem(tag + "_product")
        s_b = sem(tag + "_biased")
        ob = sb(tag + "_ob", [P, NT, D], F32, G_ + 16 * K)

        class Out(Stage):
            ready, tile = s_b, ob

            @staticmethod
            def tensor(pe):
                for hf in range(2):
                    pe.wait_ge(att.attn_ready, 7 + hf)
                    for c in range(NC):
                        for i in range(4):
                            m = pe.transpose(PS[:, 2 * hf + c, P * i:P * i + P],
                                             attn[:, 4 * hf + i, P * c:P * c + P], ident[:])
                        m.then_inc(s_t, 1)
                wo_ready(pe)
                for n in range(NT):
                    t = slice(P * n, P * n + P)
                    pe.wait_ge(s_lo, 2 * (n // 4) + 2)
                    if n >= 4:
                        pe.wait_ge(s_b, n - 3)
                    product(pe, PS[:, 4 + n % 4, 0:D], lambda c: xhi[:, c, t], lambda c: xlo[:, c, t],
                            lambda c: wo_hi[:, c, :], lambda c: wo_lo[:, c, :], NC).then_inc(s_o, 1)

            @staticmethod
            def scalar(act):
                for k in range(4):
                    hf, c = divmod(k, 2)
                    act.wait_ge(s_t, k + 1)
                    act.activation(xhi[:, c, HALF * hf:HALF * hf + HALF], PS[:, k, :], ACT.Copy).then_inc(s_hi, 1)

            @staticmethod
            def vector(dve):
                for k in range(4):
                    hf, c = divmod(k, 2)
                    dve.wait_ge(s_hi, k + 1)
                    dve.tensor_tensor(xlo[:, c, HALF * hf:HALF * hf + HALF], PS[:, k, :],
                                      xhi[:, c, HALF * hf:HALF * hf + HALF].bitcast(F32), ALU.subtract).then_inc(s_lo, 1)
                for n in range(NT):
                    dve.wait_ge(s_o, n + 1)
                    if bias is not None:
                        dve.tensor_tensor(ob[:, n, :], PS[:, 4 + n % 4, 0:D], bias[:], ALU.add).then_inc(s_b, 1)
                    else:
                        dve.tensor_copy(ob[:, n, :], PS[:, 4 + n % 4, 0:D]).then_inc(s_b, 1)
        return Out

    s_wf_ld = [sem(f"ffn0_weights_loaded{i}") for i in range(2)]
    s_wf = sem("ffn0_weights_split")
    up_raw = stage[:, 0:2048]
    CH = 512

    def flat(t):
        v = t[:]
        while v.ndim > 2:
            v = v.rearrange("p a b -> p (a b)") if v.ndim == 3 else v.rearrange("p a b c -> p (a b c)")
        return v

    f0_chunks = []
    for k in range(4):
        f0_chunks.append((0, stage[:, CH * k:CH * k + CH], flat(w_up_hi)[:, CH * k:CH * k + CH],
                          flat(w_up_lo)[:, CH * k:CH * k + CH]))
    for k in range(2):
        f0_chunks.append((1, stage[:, CH * k:CH * k + CH], flat(w_sw_hi)[:, CH * k:CH * k + CH],
                          flat(w_sw_lo)[:, CH * k:CH * k + CH]))
    for k in range(4):
        f0_chunks.append((1, stage[:, 1024 + CH * k:1024 + CH * k + CH], flat(w_dn_hi)[:, CH * k:CH * k + CH],
                          flat(w_dn_lo)[:, CH * k:CH * k + CH]))

    def split_f0(pool, v):
        if v == 0:
            pool.dma_start(stage[:, 0:2048], a["w_f0"][:, 0:2048]).then_inc(s_wf_ld[0], 16)
            return
        for n in range(2 * (v - 1), min(2 * v, len(f0_chunks))):
            piece, raw, hi, lo = f0_chunks[n]
            if n == 0:
                pool.wait_ge(s_wlo, 4)
            if n in (0, 4):
                pool.wait_ge(s_wf_ld[piece], 16)
            pool.tensor_copy(hi, raw).then_inc(s_wf, 1)
            pool.wait_ge(s_wf, 2 * n + 1)
            pool.tensor_tensor(lo, raw, hi.bitcast(F32), ALU.subtract).then_inc(s_wf, 1)
            pool.wait_ge(s_wf, 2 * n + 2)
            if n == 3:
                pool.dma_start(stage[:], a["w_f0"][:, 2048:5120]).then_inc(s_wf_ld[1], 16)

    F0_SPLIT = 20
    att0 = attention("att0", False, s_scr0, (32, 32), lambda pe: pe.wait_ge(s_vaug0, NT), HEADS, split_f0)
    stages.append(att0)
    out0 = out_projection("out0", att0, lambda pe: pe.wait_ge(s_wlo, 4), bo_b)
    stages.append(out0)
    yb = sb("yb", [P, NT, D], F32, D_)
    post0 = post_norm("post0", lambda t: out0.tile[:, t, :], lambda dve, hf: dve.wait_ge(out0.ready, 4 * hf + 4), yb)
    stages.append(post0)
    last_x = post0.x

    def before(dve, step, logit, gt, eq, n):
        lj = logit[:].unsqueeze(2).broadcast_to([P, n, 8, 8])
        li = logit[:].unsqueeze(3).broadcast_to([P, n, 8, 8])
        dve.tensor_tensor(gt[:], lj, li, ALU.is_gt).then_inc(step.sem, 1)
        dve.tensor_tensor(eq[:], lj, li, ALU.is_equal).then_inc(step.sem, 1)
        step.wait(dve, 2)
        dve.tensor_tensor(eq[:], eq[:], tri[:].unsqueeze(1).broadcast_to([P, n, 8, 8]), ALU.mult).then_inc(step.sem, 1)
        step.wait(dve, 1)
        dve.tensor_tensor(gt[:], gt[:], eq[:], ALU.add).then_inc(step.sem, 1)
        step.wait(dve, 1)

    class Steps:

        def __init__(self, s, at=0):
            self.sem, self.at = s, at

        def wait(self, eng, k):
            self.at += k
            eng.wait_ge(self.sem, self.at)

    def stack_weights(dve, step, w, st):
        dve.tensor_copy(st[:, :, 0:8], w[:]).then_inc(step.sem, 1)
        step.wait(dve, 1)
        dve.tensor_tensor(st[:, :, 32:40], w[:], st[:, :, 0:8].bitcast(F32), ALU.subtract).then_inc(step.sem, 1)
        dve.tensor_copy(st[:, :, 64:72], st[:, :, 0:8].bitcast(F32)).then_inc(step.sem, 1)
        step.wait(dve, 2)

    xn_f0 = sb("xn_f0", [P, NT, D], F32, 70 * K)
    pre_f0 = pre_norm("pre_f0", xn_f0, lambda dve, hf: dve.wait_ge(post0.x, 4 * hf + 4), keep=(res_t,))

    NQ = 2 * ROUNDS
    NK0 = NQ * N0
    s_up = sem("f0_up")
    s_hhi = sem("f0_h_hi")
    s_hlo = sem("f0_h_lo")
    s_sg = sem("f0_inner")
    s_si = sem("f0_silu")
    s_sp = sem("f0_silu_weighted")
    s_g = sem("f0_g")
    s_ghi = sem("f0_g_hi")
    s_glo = sem("f0_g_lo")
    s_dn = sem("f0_down")
    s_acc = sem("f0_sum")
    s_xh = sem("f0_x_hi")
    s_xl = sem("f0_x_lo")
    s_gm = sem("f0_gate_logits")
    s_gs = sem("f0_gate_step")
    GSTEPS = 15
    s_gb = sem("f0_base_ready")
    s_gx = sem("f0_gate_exp")
    s_gT = sem("f0_gate_transposed")
    s_gE = sem("f0_gate_evacuated")
    s_wbm = sem("f0_weight_broadcast")
    s_wbe = sem("f0_weight_ready")
    s_f0c = sem("f0_constants")
    s_wgl = sem("f0_gate_weights_loaded")

    FLAG, ULAG = 3, 4
    def gate_slot(q):
        return max(0, N0 * q - 1)

    def gate_part_slot(q, part):
        return gate_slot(q) + (part if part < 2 else 3 if q == 0 else 4)

    def gate_exp_slot(q, i):
        return gate_slot(q) + 1 + (0 if q == 0 else min(i, 2))

    def rows_slot(q):
        return gate_part_slot(q, 2) + 1

    def spread_slot(q, e):
        return rows_slot(q) + (e + 1) // 2

    def sum_slot(k):
        q, r = divmod(k - ULAG - N0 + 1, N0)
        return q if r == 0 and 0 <= q < NQ else None

    class Ffn0(Stage):
        @staticmethod
        def sync(sp):
            sp.dma_start(wg_sb[:], a["w_g0"]).then_inc(s_wgl, 16)

        @staticmethod
        def tensor(pe):
            def gate(q):
                r, hf = divmod(q, 2)
                if q == 0:
                    pe.wait_ge(s_wgl, 16)
                    pe.wait_ge(pre_f0.kept, 4)
                elif q >= 2:
                    pe.wait_ge(s_acc, 2 * (q - 1))
                if q >= 1:
                    pe.wait_ge(s_wbe, E0 * q)
                for i in range(4):
                    for c in range(NC):
                        m = pe.matmul(PS[:, 7, 8 * i:8 * i + 8], (xc_t if r else res_t)[:, c, HALF * hf + P * i:HALF * hf + P * i + P],
                                      wg_sb[:, r, c, :], start=c == 0, stop=c == NC - 1)
                m.then_inc(s_gm, 1)

            def rows(q):
                pe.wait_ge(s_gs, GSTEPS * (q + 1))
                for i in range(4):
                    m = pe.transpose(PS[0:96, 7, P * i:P * i + P], wst[:, i, :].bitcast(F32), ident[:])
                m.then_inc(s_gT, 1)

            def spread(q, e):
                n = E0 * q + e
                pe.wait_ge(s_gE, q + 1)
                if e:
                    pe.wait_ge(s_wbe, n)
                pe.matmul(PS[:, 7, :], sel[:, e, :], wt0[:, q % 2, :], start=True, stop=True).then_inc(s_wbm, 1)

            def up(k):
                q, n = divmod(k, N0)
                hf = q % 2
                if n == 0:
                    if q < 2:
                        pe.wait_ge(pre_f0.lo, 2 * hf + 2)
                    else:
                        pe.wait_ge(s_xl, 2 * (q - 1))
                if k >= 4:
                    pe.wait_ge(s_g, k - 3)
                h = slice(HALF * hf, HALF * hf + HALF)
                product(pe, PS[:, k % 4, :], lambda c: w_up_hi[:, n, c, :], lambda c: w_up_lo[:, n, c, :],
                        lambda c: xhi[:, c, h], lambda c: xlo[:, c, h], NC).then_inc(s_up, 1)

            def inner(k):
                n = k % N0
                pe.wait_ge(s_hlo, k + 1)
                if k >= 1:
                    pe.wait_ge(s_si, k)
                product(pe, PS[:, 4, :], lambda c: w_sw_hi[:, n, :], lambda c: w_sw_lo[:, n, :],
                        lambda c: h_hi[:, k % 2, :], lambda c: h_lo[:, k % 2, :], 1).then_inc(s_sg, 1)

            def down(k):
                q, n = divmod(k, N0)
                pe.wait_ge(s_glo, k + 1)
                if n == 0 and q:
                    pe.wait_ge(s_acc, 2 * q)
                for m in range(NC):
                    mm = product(pe, PS[:, 5 + m, :], lambda c: w_dn_hi[:, n, P * m:P * m + P],
                                 lambda c: w_dn_lo[:, n, P * m:P * m + P], lambda c: g_hi[:, k % 3, :],
                                 lambda c: g_lo[:, k % 3, :], 1, start=n == 0, stop=False)
                    if n == N0 - 1:
                        mm = pe.matmul(PS[:, 5 + m, :], bst[:, P * m:P * m + P], wt0[:, q % 2, :], start=False, stop=True)
                mm.then_inc(s_dn, 1)

            pe.wait_ge(s_wf, F0_SPLIT)
            for k in range(NK0 + ULAG):
                for q in range(NQ):
                    if k == gate_slot(q):
                        gate(q)
                    if k == rows_slot(q):
                        rows(q)
                    for e in range(1, E0, 2):
                        if k == spread_slot(q, e):
                            spread(q, e)
                if k < NK0:
                    up(k)
                if 1 <= k <= NK0:
                    inner(k - 1)
                for q in range(NQ):
                    for e in range(0, E0, 2):
                        if k == spread_slot(q, e):
                            spread(q, e)
                if ULAG <= k:
                    down(k - ULAG)

        @staticmethod
        def scalar(act):
            def keep_spread(k, first):
                for q in range(NQ):
                    for e in range(first, E0, 2):
                        if k == spread_slot(q, e):
                            act.wait_ge(s_wbm, E0 * q + e + 1)
                            if q >= 2:
                                act.wait_ge(s_sp, E0 * (q - 1))
                            act.activation(wb0[:, q % 2, e, :], PS[:, 7, :], ACT.Copy).then_inc(s_wbe, 1)

            for k in range(NK0 + ULAG):
                for q in range(NQ):
                    if k == rows_slot(q):
                        act.wait_ge(s_gT, q + 1)
                        if q >= 2:
                            act.wait_ge(s_dn, N0 * (q - 1))
                        act.activation(wt0[:, q % 2, :], PS[0:96, 7, :], ACT.Copy).then_inc(s_gE, 1)
                if 2 <= k <= NK0 + 1:
                    j = k - 2
                    act.wait_ge(s_sg, j + 1)
                    if j >= 2:
                        act.wait_ge(s_g, j - 1)
                        if sp_count(j - 2):
                            act.wait_ge(s_sp, sp_count(j - 2))
                    act.activation(f_s[:, j % 2, :], PS[:, 4, :], ACT.Silu, bias=b_sw[:, j % N0:j % N0 + 1])\
                       .then_inc(s_si, 1)
                keep_spread(k, 1)
                if FLAG <= k <= NK0 + FLAG - 1:
                    j = k - FLAG
                    act.wait_ge(s_g, j + 1)
                    if j >= 3:
                        act.wait_ge(s_dn, j - 2)
                    act.activation(g_hi[:, j % 3, :], f_g[:, j % 2, :], ACT.Copy).then_inc(s_ghi, 1)
                if k < NK0:
                    act.wait_ge(s_up, k + 1)
                    if k >= 2:
                        act.wait_ge(s_sg, k - 1)
                    act.activation(h_hi[:, k % 2, :], PS[:, k % 4, :], ACT.Identity, bias=b_up[:, k % N0:k % N0 + 1])\
                       .then_inc(s_hhi, 1)
                keep_spread(k, 0)
                q = sum_slot(k - 1)
                if q is not None and q < 2:
                    for c in range(NC):
                        act.wait_ge(s_acc, 2 * q + c + 1)
                        act.activation(xhi[:, c, HALF * (q % 2):HALF * (q % 2) + HALF],
                                       xc_t[:, c, HALF * (q % 2):HALF * (q % 2) + HALF], ACT.Copy).then_inc(s_xh, 1)

        @staticmethod
        def vector(dve):
            dve.memset(wst[:].bitcast(F32), 0.0).then_inc(s_f0c, 1)
            dve.tensor_copy(bst[:], bst_raw[:]).then_inc(s_f0c, 1)
            dve.wait_ge(s_f0c, 2)
            dve.tensor_tensor(bst[64:96, :], bst_raw[64:96, :], bst[64:96, :].bitcast(F32), ALU.subtract)\
               .then_inc(s_f0c, 1)
            dve.wait_ge(s_f0c, 3)

            def gate(q, part):
                r = q // 2
                at = GSTEPS * q
                lj = gl[:].unsqueeze(2).broadcast_to([P, 4, 8, 8])
                li = gl[:].unsqueeze(3).broadcast_to([P, 4, 8, 8])
                if part == 0:
                    dve.wait_ge(s_gm, q + 1)
                    if q:
                        dve.wait_ge(s_gT, q)
                    dve.tensor_tensor(gl[:], PS[:, 7, 0:32].rearrange("p (t e) -> p t e", e=8),
                                      bg_b[:, r, :].unsqueeze(1).broadcast_to([P, 4, 8]), ALU.add).then_inc(s_gs, 1)
                    dve.wait_ge(s_gs, at + 1)
                    dve.tensor_reduce(g_m[:], gl[:], AX.X, ALU.max).then_inc(s_gs, 1)
                    dve.wait_ge(s_gs, at + 2)
                    dve.tensor_tensor(g_w[:], gl[:], g_m[:].unsqueeze(2).broadcast_to([P, 4, 8]), ALU.subtract)\
                       .then_inc(s_gs, 1)
                    dve.tensor_tensor(g_gt[:], lj, li, ALU.is_gt).then_inc(s_gs, 1)
                    dve.tensor_tensor(g_eq[:], lj, li, ALU.is_equal).then_inc(s_gs, 1)
                elif part == 1:
                    dve.wait_ge(s_gs, at + 5)
                    dve.tensor_tensor(g_eq[:], g_eq[:], tri[:].unsqueeze(1).broadcast_to([P, 4, 8, 8]), ALU.mult)\
                       .then_inc(s_gs, 1)
                    dve.wait_ge(s_gs, at + 6)
                    dve.tensor_tensor(g_gt[:], g_gt[:], g_eq[:], ALU.add).then_inc(s_gs, 1)
                    dve.wait_ge(s_gs, at + 7)
                    dve.tensor_reduce(g_rank[:], g_gt[:], AX.X, ALU.add).then_inc(s_gs, 1)
                elif part == 2:
                    dve.wait_ge(s_gs, at + 8)
                    dve.wait_ge(s_gx, 4 * (q + 1))
                    dve.scalar_tensor_tensor(g_w[:], g_rank[:], E0 - 0.5, g_e[:], ALU.is_lt, ALU.mult).then_inc(s_gs, 1)
                    dve.wait_ge(s_gs, at + 9)
                    dve.tensor_reduce(g_m[:], g_w[:], AX.X, ALU.add).then_inc(s_gs, 1)
                    dve.wait_ge(s_gs, at + 10)
                    dve.reciprocal(g_r[:], g_m[:]).then_inc(s_gs, 1)
                    dve.wait_ge(s_gs, at + 11)
                    dve.tensor_tensor(gl[:], g_w[:], g_r[:].unsqueeze(2).broadcast_to([P, 4, 8]), ALU.mult).then_inc(s_gs, 1)
                    dve.wait_ge(s_gs, at + 12)
                    dve.tensor_copy(wst[:, :, 0:8], gl[:]).then_inc(s_gs, 1)
                    dve.wait_ge(s_gs, at + 13)
                    dve.tensor_tensor(wst[:, :, 32:40], gl[:], wst[:, :, 0:8].bitcast(F32), ALU.subtract).then_inc(s_gs, 1)
                    dve.tensor_copy(wst[:, :, 64:72], wst[:, :, 0:8].bitcast(F32)).then_inc(s_gs, 1)

            for k in range(NK0 + ULAG + 1):
                q = sum_slot(k - 1)
                if q is not None:
                    hf = q % 2
                    dve.wait_ge(s_dn, N0 * (q + 1))
                    if q == 0:
                        dve.wait_ge(pre_f0.kept, 4)
                    for c in range(NC):
                        h = slice(HALF * hf, HALF * hf + HALF)
                        dve.scalar_tensor_tensor(xc_t[:, c, h], PS[:, 5 + c, :], b_sd[:, c:c + 1], res_t[:, c, h],
                                                 ALU.add, ALU.add).then_inc(s_acc, 1)
                if FLAG <= k <= NK0 + FLAG - 1:
                    j = k - FLAG
                    n = j % N0
                    if n < 2:
                        dve.wait_ge(s_si, j + 1)
                        w = f_s
                    else:
                        dve.wait_ge(s_sp, sp_count(j))
                        w = f_sw
                    if j >= 2:
                        dve.wait_ge(s_ghi, j - 1)
                        dve.wait_ge(s_glo, j - 1)
                    dve.scalar_tensor_tensor(f_g[:, j % 2, :], PS[:, j % 4, :], b_up[:, n:n + 1], w[:, j % 2, :],
                                             ALU.add, ALU.mult).then_inc(s_g, 1)
                    dve.wait_ge(s_ghi, j + 1)
                    if j >= 3:
                        dve.wait_ge(s_dn, j - 2)
                    dve.tensor_tensor(g_lo[:, j % 3, :], f_g[:, j % 2, :], g_hi[:, j % 3, :].bitcast(F32), ALU.subtract)\
                       .then_inc(s_glo, 1)
                if k < NK0:
                    dve.wait_ge(s_hhi, k + 1)
                    if k >= 2:
                        dve.wait_ge(s_sg, k - 1)
                    dve.scalar_tensor_tensor(h_lo[:, k % 2, :], PS[:, k % 4, :], b_up[:, k % N0:k % N0 + 1],
                                             h_hi[:, k % 2, :].bitcast(F32), ALU.add, ALU.subtract).then_inc(s_hlo, 1)
                q = sum_slot(k - 1)
                if q is not None and q < 2:
                    hf = q % 2
                    for c in range(NC):
                        h = slice(HALF * hf, HALF * hf + HALF)
                        dve.wait_ge(s_xh, 2 * q + c + 1)
                        dve.tensor_tensor(xlo[:, c, h], xc_t[:, c, h], xhi[:, c, h].bitcast(F32), ALU.subtract)\
                           .then_inc(s_xl, 1)
                for q in range(NQ):
                    for part in range(3):
                        if k == gate_part_slot(q, part):
                            gate(q, part)
                if k in A1_SLOTS:
                    attn1_hi(dve, A1_SLOTS.index(k))

        @staticmethod
        def gpsimd(pool):
            pool.wait_ge(post0.x, NT)
            pool.memset(g_base[:], float(np.e)).then_inc(s_gb, 1)
            for k in range(NK0 + 2):
                j = k - 2
                if j >= 0 and j % N0 >= 2:
                    q, n = divmod(j, N0)
                    pool.wait_ge(s_si, j + 1)
                    pool.wait_ge(s_wbe, E0 * q + n - 1)
                    if j >= 2:
                        pool.wait_ge(s_g, j - 1)
                    pool.tensor_tensor(f_sw[:, j % 2, :], f_s[:, j % 2, :], wb0[:, q % 2, n - 2, :], ALU.mult)\
                        .then_inc(s_sp, 1)
                for q in range(NQ):
                    for i in range(4):
                        if k == gate_exp_slot(q, i):
                            pool.wait_ge(s_gb, 1)
                            pool.wait_ge(s_gs, GSTEPS * q + 3)
                            if q:
                                pool.wait_ge(s_gs, GSTEPS * (q - 1) + 9)
                            pool.tensor_tensor(g_e[:, i, :], g_base[:, i, :], g_w[:, i, :], ALU.pow).then_inc(s_gx, 1)
                if k == 6:
                    attn1_load(pool)
                if k - 3 in A1_SLOTS:
                    attn1_lo(pool, A1_SLOTS.index(k - 3))

    def sp_count(k):
        q, n = divmod(k, N0)
        return E0 * q + max(0, n - 1)

    s_a1_ld = sem("attn1_weights_loaded")
    s_a1h = sem("attn1_weights_hi")
    s_a1 = sem("attn1_weights_lo")
    A1 = [(flat(w1q_hi), flat(w1q_lo), 1024), (flat(w1k_hi), flat(w1k_lo), 512), (flat(w1v_hi), flat(w1v_lo), 128),
          (flat(wo_hi), flat(wo_lo), 512)]
    a1_chunks = []
    at = 0
    for hi, lo, n in A1:
        for c in range(0, n, 512):
            w = min(512, n - c)
            a1_chunks.append((at, w, hi[:, c:c + w], lo[:, c:c + w]))
            at += w
    s_rope = sem("rope_loaded")

    A1_SLOTS = (7, 8, 16, 18, 24)
    assert len(A1_SLOTS) == len(a1_chunks)

    def attn1_load(pool):
        pool.wait_ge(s_wf, F0_SPLIT)
        pool.dma_start(stage[:, 0:at], a["w_a1"]).then_inc(s_a1_ld, 16)
        pool.wait_ge(post0.x, NT)
        pool.dma_start(rope[:], a["rope"]).then_inc(s_rope, 16)

    def attn1_hi(dve, n):
        c, w, hi, lo = a1_chunks[n]
        if n == 0:
            dve.wait_ge(s_a1_ld, 16)
            dve.wait_ge(post0.x, NT)
        dve.tensor_copy(hi, stage[:, c:c + w]).then_inc(s_a1h, 1)

    def attn1_lo(pool, n):
        c, w, hi, lo = a1_chunks[n]
        pool.wait_ge(s_a1h, n + 1)
        pool.tensor_tensor(lo, stage[:, c:c + w], hi.bitcast(F32), ALU.subtract).then_inc(s_a1, 1)

    def tokens_again(tag, src_t, wait_src):
        s_t = sem(tag + "_back")

        class Back(Stage):
            ready = s_t

            @staticmethod
            def tensor(pe):
                for t in range(NT):
                    if t % 4 == 0:
                        wait_src(pe, t // 4)
                    for c in range(NC):
                        m = pe.transpose(PS[:, t // 2, D * (t % 2) + P * c:D * (t % 2) + P * c + P],
                                         src_t[:, c, P * t:P * t + P], ident[:])
                    m.then_inc(s_t, 1)
        return Back

    def bank_tile(t):
        return PS[:, t // 2, D * (t % 2):D * (t % 2) + D]

    if UPTO >= 2:
        stages.append(pre_f0)
        stages.append(Ffn0)
        back0 = tokens_again("f0", xc_t, lambda pe, hf: pe.wait_ge(s_acc, 2 * NQ))
        stages.append(back0)
        yb_f0 = sb("yb_f0", [P, NT, D], F32, 70 * K)
        post_f0 = post_norm("post_f0", bank_tile, lambda dve, hf: dve.wait_ge(back0.ready, 4 * hf + 4), yb_f0)
        stages.append(post_f0)
        last_x = post_f0.x

    units1 = [("q", 0, 0), ("q", 0, 1), ("k", 0, 0), ("k", 0, 1), ("q", 1, 0), ("q", 1, 1)]
    xn1 = sb("xn1", [P, NT, D], F32, 70 * K)
    pre1 = pre_norm("pre1", xn1, lambda dve, hf: dve.wait_ge(post_f0.x, 4 * hf + 4))
    part_of = {("q", 0): 0, ("k", 0): 1, ("q", 1): 2}
    split1 = split_parts("qk1", [(parts[part_of[op, m]], hf) for op, m, hf in units1])
    s_qk1 = sem("qk1_product")
    s_cos, s_sin = sem("qk1_cos"), sem("qk1_sin")
    s_v1 = sem("v1_product")
    s_vaug1 = sem("v1_ready")
    s_scr1 = [sem(f"qk1_in_scratch{m}") for m in range(2)]
    s_a1c = sem("attn1_constants")

    class Project1(Stage):
        @staticmethod
        def tensor(pe):
            pe.wait_ge(s_a1, len(a1_chunks))
            for n, (op, m, hf) in enumerate(units1):
                pe.wait_ge(pre1.lo, 2 * hf + 2)
                if n >= 2:
                    pe.wait_ge(s_sin, n - 1)
                h = slice(HALF * hf, HALF * hf + HALF)
                for r in range(2):
                    if op == "q":
                        hi, lo = (lambda c: w1q_hi[:, r, c, P * m:P * m + P]), (lambda c: w1q_lo[:, r, c, P * m:P * m + P])
                    else:
                        hi, lo = (lambda c: w1k_hi[:, r, c, :]), (lambda c: w1k_lo[:, r, c, :])
                    mm = product(pe, PS[:, 4 + 2 * (n % 2) + r, :], hi, lo, lambda c: xhi[:, c, h], lambda c: xlo[:, c, h], NC)
                mm.then_inc(s_qk1, 1)
            for n in range(NT):
                t = slice(P * n, P * n + P)
                mm = product(pe, PS[:, 2, 64 * n:64 * n + 64], lambda c: xhi[:, c, t], lambda c: xlo[:, c, t],
                             lambda c: w1v_hi[:, c, :], lambda c: w1v_lo[:, c, :], NC)
            mm.then_inc(s_v1, 1)

        @staticmethod
        def scalar(act):
            for n in range(len(units1)):
                split1.act_first(act, n)
                if n >= 1:
                    split1.act_second(act, n - 1)
            split1.act_second(act, len(units1) - 1)

        @staticmethod
        def gpsimd(pool):
            pool.wait_ge(post_f0.x, NT)
            pool.memset(vaug[:], 1.0).then_inc(s_a1c, 1)
            pool.wait_ge(s_a1c, 1)
            pool.memset(ka[0][96:99, :, :], 1.0).then_inc(s_a1c, 1)
            pool.wait_ge(s_a1c, 2)
            for n in range(len(units1)):
                pool.wait_ge(s_sin, n + 1)
                split1.free(pool, n)
                pool.tensor_tensor(qf[:, n % 2, :], rot[:, n % 2, 0, :], rot[:, n % 2, 1, :], ALU.add)\
                    .then_inc(split1.f, 1)

        @staticmethod
        def vector(dve):
            dve.wait_ge(s_rope, 16)
            for n, (op, m, hf) in enumerate(units1):
                dve.wait_ge(s_qk1, n + 1)
                if n >= 2:
                    dve.wait_ge(split1.f, n - 1)
                h = slice(HALF * hf, HALF * hf + HALF)
                dve.tensor_tensor(rot[:, n % 2, 0, :], PS[:, 4 + 2 * (n % 2), :], rope[:, 0, h], ALU.mult).then_inc(s_cos, 1)
                dve.tensor_tensor(rot[:, n % 2, 1, :], PS[:, 5 + 2 * (n % 2), :], rope[:, 1, h], ALU.mult).then_inc(s_sin, 1)
                if n >= 1:
                    split1.dve_first(dve, n - 1)
                if n >= 2:
                    split1.dve_second(dve, n - 2)
            n = len(units1)
            split1.dve_first(dve, n - 1)
            split1.dve_second(dve, n - 2)
            split1.dve_second(dve, n - 1)
            dve.wait_ge(s_v1, 1)
            dve.wait_ge(s_a1c, 2)
            dve.tensor_copy(vaug[:, :, 0:GROUPS * VW].rearrange("p t (h w) -> p t h w", w=VW)[:, :, :, 0:HD],
                            PS[:, 2, :].rearrange("p (t h w) -> p t h w", t=NT, w=HD)).then_inc(s_vaug1, 1)

        @staticmethod
        def sync(sp):
            for i, (scr, m, n) in enumerate(((scr_q, 0, 2), (scr_k, 0, 4), (scr_q, 1, 6))):
                sp.wait_ge(split1.p3, n)
                sp.dma_start(scr[m].rearrange("s p t -> p s t"), parts[i][:]).then_inc(s_scr1[m], 16)

    s_w1_ld = [sem(f"ffn1_weights_loaded{b}") for b in range(2)]
    s_w1h = sem("ffn1_weights_hi")
    s_w1l = sem("ffn1_weights_lo")

    def load_expert(eng, e):
        if e >= 2:
            eng.wait_ge(s_w1l, 3 * (e - 1))
        eng.dma_start(raw1[e % 2][:], a["w_f1"][e]).then_inc(s_w1_ld[e % 2], 16)

    def split_hi(eng, e, piece, on_scalar):
        c = slice(1024 * piece, 1024 * piece + 1024)
        if piece == 0:
            eng.wait_ge(s_w1_ld[e % 2], 16 * (e // 2 + 1))
        src, dst = raw1[e % 2][:, c], w1[e % 2][0][:, piece, :]
        if on_scalar:
            eng.activation(dst, src, ACT.Copy).then_inc(s_w1h, 1)
        else:
            eng.tensor_copy(dst, src).then_inc(s_w1h, 1)

    def split_lo(pool, e, piece):
        c = slice(1024 * piece, 1024 * piece + 1024)
        pool.wait_ge(s_w1h, 3 * e + piece + 1)
        pool.tensor_tensor(w1[e % 2][1][:, piece, :], raw1[e % 2][:, c], w1[e % 2][0][:, piece, :].bitcast(F32),
                           ALU.subtract).then_inc(s_w1l, 1)

    def early_experts(pool, v):
        if v == 0:
            pool.wait_ge(s_a1, len(a1_chunks))
            load_expert(pool, 0)
        elif v == 1:
            pool.wait_ge(s_scr1[0], 32)
            pool.wait_ge(s_scr1[1], 16)
            load_expert(pool, 1)
        if v >= 2:
            split_hi(pool, (v - 2) // 3, (v - 2) % 3, False)
            split_lo(pool, (v - 2) // 3, (v - 2) % 3)

    if UPTO >= 3:
        stages.append(pre1)
        stages.append(Project1)
        att1 = attention("att1", True, s_scr1, (32, 16), lambda pe: pe.wait_ge(s_vaug1, 1), GROUPS, early_experts)
        stages.append(att1)
        out1 = out_projection("out1", att1, lambda pe: pe.wait_ge(s_a1, len(a1_chunks)), None)
        stages.append(out1)
        yb1 = sb("yb1", [P, NT, D], F32, 70 * K)
        post1 = post_norm("post1", lambda t: out1.tile[:, t, :], lambda dve, hf: dve.wait_ge(out1.ready, 4 * hf + 4), yb1)
        stages.append(post1)
        last_x = post1.x

    NK1 = E1 * 2 * I1
    DLAG = 2
    if UPTO >= 4:
        xn_f1 = sb("xn_f1", [P, NT, D], F32, 84 * K)
        pre_f1 = pre_norm("pre_f1", xn_f1, lambda dve, hf: dve.wait_ge(post1.x, 4 * hf + 4), keep=(x1_t,))
    s_rwl = sem("router_loaded")
    s_rm = sem("router_logits")
    s_rs = sem("router_step")
    RSTEPS = 17
    s_rT = sem("router_transposed")
    s_rE = sem("router_evacuated")
    s_w1m = sem("f1_weight_broadcast")
    s_w1a, s_w1d = sem("f1_weight_ready_a"), sem("f1_weight_ready_d")
    s_f1c = sem("f1_constants")
    s_ga = sem("f1_gate")
    s_u = sem("f1_up")
    s_f1s = sem("f1_silu")
    s_f1p = sem("f1_silu_weighted")
    s_f1g = sem("f1_g")
    s_f1h = sem("f1_g_hi")
    s_f1l = sem("f1_g_lo")
    s_f1d = sem("f1_down")
    s_y1 = sem("f1_sum_evacuated")

    class Router(Stage):

        @staticmethod
        def sync(sp):
            sp.wait_ge(post1.x, NT)
            sp.dma_start(rw_sb[:], a["w_r1"]).then_inc(s_rwl, 16)

        @staticmethod
        def tensor(pe):
            pe.wait_ge(s_rwl, 16)
            pe.wait_ge(pre_f1.kept, 4)
            for t in range(NT):
                for c in range(NC):
                    m = pe.matmul(PS[:, 4, 8 * t:8 * t + 8], x1_t[:, c, P * t:P * t + P], rw_sb[:, c, :],
                                  start=c == 0, stop=c == NC - 1)
            m.then_inc(s_rm, 1)
            pe.wait_ge(s_rs, RSTEPS)
            pe.wait_ge(pre_f1.lo, 4)
            for hf in range(2):
                for i in range(4):
                    m = pe.transpose(PS[0:96, 5 + hf, P * i:P * i + P], wst1[:, 4 * hf + i, :].bitcast(F32), ident[:])
                m.then_inc(s_rT, 1)
            for n in range(2 * E1):
                e, hf = divmod(n, 2)
                pe.wait_ge(s_rE, hf + 1)
                if n >= 4:
                    k = (n - 4) // 2 + 1
                    pe.wait_ge(s_w1a if n % 2 == 0 else s_w1d, k)
                pe.matmul(PS[:, n % 4, :], sel[:, e, :], wt1[:, HALF * hf:HALF * hf + HALF], start=True, stop=True)\
                  .then_inc(s_w1m, 1)

        @staticmethod
        def scalar(act):
            act.wait_ge(s_rs, 3)
            act.activation(r_e[:], r_x[:], ACT.Exp).then_inc(s_rs, 1)
            for hf in range(2):
                act.wait_ge(s_rT, hf + 1)
                act.activation(wt1[:, HALF * hf:HALF * hf + HALF], PS[0:96, 5 + hf, :], ACT.Copy).then_inc(s_rE, 1)
            for n in range(0, 2 * E1, 2):
                act.wait_ge(s_w1m, n + 1)
                act.activation(wb1[:, n // 2, 0:HALF], PS[:, n % 4, :], ACT.Copy).then_inc(s_w1a, 1)

        @staticmethod
        def vector(dve):
            st = Steps(s_rs)
            dve.memset(wst1[:].bitcast(F32), 0.0).then_inc(s_f1c, 1)
            dve.wait_ge(s_rm, 1)
            dve.tensor_copy(r_l[:], PS[:, 4, 0:64].rearrange("p (t e) -> p t e", e=8)).then_inc(s_rs, 1)
            st.wait(dve, 1)
            dve.tensor_reduce(r_m[:], r_l[:], AX.X, ALU.max).then_inc(s_rs, 1)
            st.wait(dve, 1)
            dve.tensor_tensor(r_x[:], r_l[:], r_m[:].unsqueeze(2).broadcast_to([P, NT, 8]), ALU.subtract)\
               .then_inc(s_rs, 1)
            st.wait(dve, 2)
            dve.tensor_reduce(r_m[:], r_e[:], AX.X, ALU.add).then_inc(s_rs, 1)
            st.wait(dve, 1)
            dve.reciprocal(r_s[:], r_m[:]).then_inc(s_rs, 1)
            st.wait(dve, 1)
            dve.tensor_tensor(r_p[:], r_e[:], r_s[:].unsqueeze(2).broadcast_to([P, NT, 8]), ALU.mult).then_inc(s_rs, 1)
            st.wait(dve, 1)
            lj = r_p[:].unsqueeze(2).broadcast_to([P, NT, 8, 8])
            before(dve, st, r_p, r_gt, r_eq, NT)
            dve.tensor_tensor(r_gt[:], r_gt[:], lj, ALU.mult).then_inc(s_rs, 1)
            st.wait(dve, 1)
            dve.tensor_reduce(r_x[:], r_gt[:], AX.X, ALU.add).then_inc(s_rs, 1)
            st.wait(dve, 1)
            dve.scalar_tensor_tensor(r_w[:], r_x[:], TOP_P, r_p[:], ALU.is_le, ALU.mult).then_inc(s_rs, 1)
            st.wait(dve, 1)
            dve.wait_ge(s_f1c, 1)
            stack_weights(dve, st, r_w, wst1)
            assert st.at == RSTEPS, st.at
            for n in range(1, 2 * E1, 2):
                dve.wait_ge(s_w1m, n + 1)
                dve.tensor_copy(wb1[:, n // 2, HALF:T], PS[:, n % 4, :]).then_inc(s_w1d, 1)

    class Ffn1(Stage):
        @staticmethod
        def tensor(pe):
            def gate_up(k):
                e, r = divmod(k, 2 * I1)
                hf, i = divmod(r, I1)
                h = slice(HALF * hf, HALF * hf + HALF)
                if r == 0:
                    pe.wait_ge(s_w1l, 3 * e + 3)
                hi, lo = w1[e % 2]
                for j, (s_done, bank, s_used) in enumerate(((s_ga, 4, s_f1s), (s_u, 6, s_f1g))):
                    if k >= 2:
                        pe.wait_ge(s_used, k - 1)
                    elif k == 0:
                        pe.wait_ge(s_w1a, E1)
                        pe.wait_ge(s_w1d, E1)
                        pe.wait_ge(s_rE, 2)
                    product(pe, PS[:, bank + k % 2, :], lambda c: hi[:, j, 512 * c + P * i:512 * c + P * i + P],
                            lambda c: lo[:, j, 512 * c + P * i:512 * c + P * i + P],
                            lambda c: xhi[:, c, h], lambda c: xlo[:, c, h], NC).then_inc(s_done, 1)

            def down(k):
                e, r = divmod(k, 2 * I1)
                hf, i = divmod(r, I1)
                hi, lo = w1[e % 2]
                pe.wait_ge(s_f1l, k + 1)
                for m in range(NC):
                    mm = product(pe, PS[:, 2 * hf + m, :], lambda c: hi[:, 2, D * i + P * m:D * i + P * m + P],
                                 lambda c: lo[:, 2, D * i + P * m:D * i + P * m + P],
                                 lambda c: m_ghi[:, k % 3, :], lambda c: m_glo[:, k % 3, :], 1,
                                 start=e == 0 and i == 0, stop=e == E1 - 1 and i == I1 - 1)
                mm.then_inc(s_f1d, 1)

            for k in range(NK1 + DLAG):
                if k < NK1:
                    gate_up(k)
                if k >= DLAG:
                    down(k - DLAG)

        @staticmethod
        def scalar(act):
            for k in range(NK1 + 1):
                if k < NK1:
                    act.wait_ge(s_ga, k + 1)
                    if k >= 3:
                        act.wait_ge(s_f1p, k - 2)
                    act.activation(m_s[:, k % 3, :], PS[:, 4 + k % 2, :], ACT.Silu).then_inc(s_f1s, 1)
                if k >= 1:
                    j = k - 1
                    act.wait_ge(s_f1g, j + 1)
                    if j >= 3:
                        act.wait_ge(s_f1d, j - 2)
                    act.activation(m_ghi[:, j % 3, :], m_g[:, j % 2, :], ACT.Copy).then_inc(s_f1h, 1)
                e, r = divmod(k, 2 * I1)
                if e + 1 < E1 and e >= 1 and r in (3, 5, 7):
                    piece = (r - 3) // 2
                    act.wait_ge(s_f1d, 2 * I1 * e)
                    split_hi(act, e + 1, piece, True)
            for hf in range(2):
                act.wait_ge(s_f1d, NK1 - (I1 if hf == 0 else 0))
                act.activation(y1_t[:, 0, HALF * hf:HALF * hf + HALF], PS[:, 2 * hf, :], ACT.Copy).then_inc(s_y1, 1)
                act.activation(y1_t[:, 1, HALF * hf:HALF * hf + HALF], PS[:, 2 * hf + 1, :], ACT.Copy).then_inc(s_y1, 1)

        @staticmethod
        def vector(dve):
            for k in range(NK1):
                dve.wait_ge(s_u, k + 1)
                dve.wait_ge(s_f1p, k + 1)
                if k >= 2:
                    dve.wait_ge(s_f1h, k - 1)
                    dve.wait_ge(s_f1l, k - 1)
                dve.tensor_tensor(m_g[:, k % 2, :], PS[:, 6 + k % 2, :], m_sw[:, k % 3, :], ALU.mult).then_inc(s_f1g, 1)
                dve.wait_ge(s_f1h, k + 1)
                if k >= 3:
                    dve.wait_ge(s_f1d, k - 2)
                dve.tensor_tensor(m_glo[:, k % 3, :], m_g[:, k % 2, :], m_ghi[:, k % 3, :].bitcast(F32), ALU.subtract)\
                   .then_inc(s_f1l, 1)

        @staticmethod
        def gpsimd(pool):
            pool.wait_ge(s_w1a, E1)
            pool.wait_ge(s_w1d, E1)
            for k in range(NK1):
                e, r = divmod(k, 2 * I1)
                if r == 0 and e == 0:
                    load_expert(pool, 2)
                if r == 0 and 1 <= e and e + 2 < E1:
                    load_expert(pool, e + 2)
                pool.wait_ge(s_f1s, k + 1)
                if k >= 3:
                    pool.wait_ge(s_f1g, k - 2)
                pool.tensor_tensor(m_sw[:, k % 3, :], m_s[:, k % 3, :],
                                   wb1[:, e, HALF * (r // I1):HALF * (r // I1) + HALF], ALU.mult).then_inc(s_f1p, 1)
                if e + 1 < E1 and e >= 1 and r in (3, 5, 7):
                    split_lo(pool, e + 1, (r - 3) // 2)

    if UPTO >= 4:
        stages.append(pre_f1)
        stages.append(Router)
        stages.append(Ffn1)
        back1 = tokens_again("f1", y1_t, lambda pe, hf: pe.wait_ge(s_y1, 4))
        stages.append(back1)
        yb_f1 = sb("yb_f1", [P, NT, D], F32, 84 * K)
        post_f1 = post_norm("post_f1", bank_tile, lambda dve, hf: dve.wait_ge(back1.ready, 4 * hf + 4), yb_f1)
        stages.append(post_f1)
        last_x = post_f1.x

    s_out = sem("out_stored")

    class Store(Stage):
        @staticmethod
        def sync(sp):
            for hf in range(2):
                sp.wait_ge(last_x, 4 * hf + 4)
                sp.dma_start(out.rearrange("(t p) d -> p t d", p=P)[:, 4 * hf:4 * hf + 4, :],
                             x_res[:, 4 * hf:4 * hf + 4, :]).then_inc(s_out, 16)
            sp.wait_ge(s_out, 32)

    stages.append(Store)

    block = ctx.enter_context(nc.Block())

    @block.sync
    def _(sp):
        for stage_of in stages:
            stage_of.sync(sp)

    @block.gpsimd
    def _(pool):
        for stage_of in stages:
            stage_of.gpsimd(pool)

    @block.scalar
    def _(act):
        for stage_of in stages:
            stage_of.scalar(act)

    @block.vector
    def _(dve):
        for stage_of in stages:
            stage_of.vector(dve)

    @block.tensor
    def _(pe):
        for stage_of in stages:
            stage_of.tensor(pe)


def host(inputs):
    f = lambda n: np.ascontiguousarray(np.asarray(inputs[n]))
    A = "L0_attn_"
    d = {"x": f(A + "x").reshape(T, D)}
    d["w_attn0"] = np.stack([f(A + "W" + m).T for m in "qkvo"])
    d["lora"] = np.stack([np.stack([f(A + "A" + m).T for m in "qkvo"]), np.stack([f(A + "B" + m) for m in "qkvo"])])
    d["bqk"] = np.stack([f(A + "b" + m).reshape(NC, P).T for m in "qk"], axis=1)
    d["bvo"] = np.stack([f(A + "bv"), f(A + "bo")])
    d["ident"] = np.eye(P, dtype=np.float32)
    i = np.arange(P)
    later = (i[None, :] > i[:, None])
    d["masks"] = np.ascontiguousarray(np.stack([np.where(later, BIG, 0), np.where(later.T, BIG, 0)], 1).astype(np.float32))
    j = np.arange(8)
    d["tri"] = np.ascontiguousarray(np.broadcast_to((j[None, :] < j[:, None]).astype(np.float32), (P, 8, 8)))
    chunk = lambda w: w.reshape(-1, P, w.shape[-1]).transpose(1, 0, 2)
    F = "L0_ffn_"
    wsu, wsd = f(F + "Wsu"), f(F + "Wsd")
    up = [wsu[:, :P], wsu[:, P:]] + list(f(F + "Wup"))
    sw = [f(F + "Wsa")] * 2 + list(f(F + "Wsw"))
    dn = [wsd[:P], wsd[P:]] + list(f(F + "Wdn"))
    d["w_f0"] = np.concatenate([np.stack([chunk(w) for w in up], 1).reshape(P, -1),
                                np.stack(sw, 1).reshape(P, -1), np.stack(dn, 1).reshape(P, -1)], 1)
    d["b_up0"] = np.concatenate([f(F + "bsu").reshape(2, P), f(F + "bup")]).T
    d["b_sw0"] = np.concatenate([np.stack([f(F + "bsa")] * 2), f(F + "bsw")]).T
    d["b_sd0"] = f(F + "bsd").reshape(NC, P).T
    d["b_g0"] = f(F + "bg")[None]
    b = np.zeros((96, D), np.float32)
    for r in (0, 32, 64):
        b[r:r + E0] = f(F + "bdn")
    d["b_dn0"] = b
    d["w_g0"] = f(F + "Wg").reshape(ROUNDS, NC, P, 8).transpose(2, 0, 1, 3)
    d["sel"] = np.zeros((96, 8, P), np.float32)
    for e in range(8):
        d["sel"][[e, 32 + e], e] = 1
    B = "L1_attn_"
    turn = np.arange(D) // HD * HD + (np.arange(D) + HD // 2) % HD
    wq, wk, wv, wo = (f(B + "W" + m) for m in "qkvo")
    wk2 = np.concatenate([wk, wk], 1)
    cat = [wq, wq[:, turn], wk2, wk2[:, turn[:P]], wv, wo]
    d["w_a1"] = np.concatenate([chunk(w).reshape(P, -1) for w in cat], 1)
    inv = np.power(np.float32(10000), (np.float32(-2) * np.arange(HD // 2, dtype=np.float32) / np.float32(HD)))
    ang = np.arange(T, dtype=np.float32)[:, None] * inv[None].astype(np.float32)
    cos, sin = np.tile(np.cos(ang), (1, 2)).T, np.tile(np.sin(ang), (1, 2)).T
    sin = np.concatenate([-sin[:HD // 2], sin[HD // 2:]])
    d["rope"] = np.stack([np.tile(cos, (P // HD, 1)), np.tile(sin, (P // HD, 1))], 1).astype(np.float32)
    M = "L1_ffn_"
    d["w_r1"] = chunk(f(M + "router_w").T)
    gw, uw, dw = f(M + "gate_w"), f(M + "up_w"), f(M + "down_w")
    d["w_f1"] = np.stack([np.concatenate([chunk(gw[e].T).reshape(P, -1), chunk(uw[e].T).reshape(P, -1),
                                          chunk(dw[e].T).reshape(P, -1)], 1) for e in range(E1)])
    return {k: np.ascontiguousarray(v) for k, v in d.items()}


def kernel(**inputs):
    import concourse.bacc as _bacc
    from concourse.bass_utils import run_bass_kernel_spmd as _run

    arrays = host(inputs)
    nc = _bacc.Bacc("TRN2", target_bir_lowering=False, num_devices=1)
    aps = {k: nc.dram_tensor("in_" + k, v.shape, mybir.dt.from_np(v.dtype), kind="ExternalInput").ap()
           for k, v in arrays.items()}
    out = nc.dram_tensor("out_x", [T, D], F32, kind="ExternalOutput").ap()
    program(nc, aps, out)
    r = _run(nc, [{"in_" + k: v for k, v in arrays.items()}], core_ids=[0])
    return r.results[0]["out_x"].reshape(1, T, D)
```

```python
from contextlib import ExitStack

import numpy as np

import concourse.bass as bass
from concourse import mybir

F32 = mybir.dt.float32
F32R = mybir.dt.float32r
BF16 = mybir.dt.bfloat16
ALU = mybir.AluOpType
ACT = mybir.ActivationFunctionType
AX = mybir.AxisListType

P = 128
T = 1024
NT = T // P
HALF = 512
D = 256
NC = D // P
HEADS, HD = 16, 16
GROUPS, GH = 4, 4
PARTS = 3
Q_SLOT = [0, 0, 0, 1, 1, 2]
K_SLOT = [0, 1, 2, 0, 1, 0]
SLOTS = len(Q_SLOT)
KS = SLOTS * HD
KM = KS + PARTS
VW = HD + 1
BIG = -3.0e38
EPS = 1e-5
N0 = 8
E0 = 6
ROUNDS = 2
E1 = 8
I1 = 512 // P
TOP_P = 0.9
ARENA = 212480
AHEAD = 3
EARLY0, EARLY1 = 17, 30
LEAD = 12


def program(nc, a, out):
    ctx = ExitStack()
    with ctx:
        ctx.enter_context(nc.sbuf_tensor("arena", [P, ARENA], mybir.dt.uint8))
        build(nc, a, out, ctx)


def build(nc, a, out, ctx):
    K = 1024
    base = nc.sbuf_base - ARENA

    def sb(name, shape, dt, at):
        size = int(np.prod(shape[1:])) * (2 if dt == BF16 else 4)
        assert at % 32 == 0 and at + size <= ARENA, (name, at, size)
        return nc.alloc_sbuf_tensor_at(name, shape, dt, offset=base + at)

    A_, C_, D_, E_, F_, G_, H_, I_, J_ = (0, 24 * K, 56 * K, 80 * K, 96 * K, 105 * K, 129 * K, 177 * K, 189 * K)
    x_res = sb("x_res", [P, NT, D], F32, A_)
    xhi = sb("xhi", [P, NC, T], F32R, A_ + 8 * K)
    xlo = sb("xlo", [P, NC, T], F32R, A_ + 16 * K)
    qa = [sb(f"qa{i}", [P, 2, GH, HALF], BF16, C_ + 8 * K * i) for i in range(2)]
    ka = [sb(f"ka{i}", [P, GH, T], BF16, C_ + 16 * K + 8 * K * i) for i in range(2)]
    qa2 = sb("qa2", [P, 2, GH, HALF], BF16, C_ + 24 * K)
    parts = [sb(f"parts{i}", [P, PARTS, T], BF16, D_ + 6 * K * i) for i in range(4)]
    qf = sb("qf", [P, 2, HALF], F32, E_)
    qd = sb("qd", [P, 2, HALF], F32, E_ + 4 * K)
    rot = sb("rot", [P, 2, 2, HALF], F32, E_ + 8 * K)
    o_t = sb("o_t", [P, 2, HALF], F32, E_)
    attn = sb("attn", [P, NT, D], F32, E_ + 4 * K)
    vaug = sb("vaug", [P, NT, 288], F32, F_)
    pt = sb("pt", [P, 6, 2, HALF], F32, G_)
    wqkv_hi = sb("wqkv_hi", [P, 3, NC, D], F32R, G_)
    wqkv_lo = sb("wqkv_lo", [P, 3, NC, D], F32R, G_ + 6 * K)
    wraw = sb("wraw", [P, 4, NC, D], F32, H_)
    weff = sb("weff", [P, 4, NC, D], F32, H_ + 8 * K)
    lora = sb("lora", [16, 2, 4, D], F32, H_ + 16 * K)
    stage = sb("stage", [P, 3072], F32, I_)
    jo = [J_]

    def small(name, shape, dt):
        t = sb(name, shape, dt, jo[0])
        jo[0] += -(-int(np.prod(shape[1:])) * (2 if dt == BF16 else 4) // 32) * 32
        return t

    ident = small("ident", [P, P], F32)
    ident_b = small("ident_b", [P, P], BF16)
    wo_hi = small("wo_hi", [P, NC, D], F32R)
    wo_lo = small("wo_lo", [P, NC, D], F32R)
    mask_raw = small("mask_raw", [P, 2, P], F32)
    mask_b = small("mask_b", [P, 2, P], BF16)
    tri = small("tri", [P, 8, 8], F32)
    bqk = small("bqk", [P, 2, NC], F32)
    bv_b = small("bv_b", [P, D], F32)
    bo_b = small("bo_b", [96, D], F32)
    bo_st = small("bo_st", [96, D], F32R)
    mhalf = small("mhalf", [P, NT], F32)
    stats = small("stats", [P, NT, 6], F32)
    mv = small("mv", [P, NT, 2], F32)
    rstd = small("rstd", [P, NT], F32)
    nmean = small("nmean", [P, NT], F32)
    mx = small("mx", [P, 2, 16, 2], F32)
    nmf = small("nmf", [P, 2, 16], F32)
    nmd = small("nmd", [P, 2, 16], F32)
    nmp = small("nmp", [P, 2, PARTS, 16], BF16)
    nmt = small("nmt", [48, 2, P], BF16)
    rden = small("rden", [P, 2, 4, GH], F32)
    sel = small("sel", [96, 8, P], F32R)
    bst = small("bst", [96, D], F32R)
    bst_raw = small("bst_raw", [96, D], F32)
    b_up = small("b_up", [P, N0], F32)
    b_sw = small("b_sw", [P, N0], F32)
    b_sd = small("b_sd", [P, NC], F32)
    bg_b = small("bg_b", [P, ROUNDS, 8], F32)
    sel_raw = sb("sel_raw", [96, 8, P], F32, H_ + 28 * K)
    w_up_hi, w_up_lo = (sb(f"w_up_{i}", [P, N0, NC, P], F32R, H_ + 20 * K * j) for j, i in enumerate(("hi", "lo")))
    w_sw_hi, w_sw_lo = (sb(f"w_sw_{i}", [P, N0, P], F32R, H_ + 8 * K + 20 * K * j) for j, i in enumerate(("hi", "lo")))
    w_dn_hi, w_dn_lo = (sb(f"w_dn_{i}", [P, N0, D], F32R, H_ + 12 * K + 20 * K * j) for j, i in enumerate(("hi", "lo")))
    wg_sb = small("wg_sb", [P, ROUNDS, NC, 8], F32)
    res_t = sb("res_t", [P, NC, T], F32, C_)
    xc_t = sb("xc_t", [P, NC, T], F32, C_ + 8 * K)
    wb0 = sb("wb0", [P, 2, E0, HALF], F32, C_ + 16 * K)
    wt0 = sb("wt0", [96, 2, HALF], F32R, 64 * K)
    wst = sb("wst", [P, 4, 96], F32R, 68 * K)
    f_s = sb("f_s", [P, 2, HALF], F32, 70 * K)
    f_sw = sb("f_sw", [P, 2, HALF], F32, 74 * K)
    f_g = sb("f_g", [P, 2, HALF], F32, 78 * K)
    h_hi = sb("h_hi", [P, 2, HALF], F32R, 82 * K)
    h_lo = sb("h_lo", [P, 2, HALF], F32R, 86 * K)
    g_hi = sb("g_hi", [P, 3, HALF], F32R, 90 * K)
    g_lo = sb("g_lo", [P, 3, HALF], F32R, 96 * K)
    gate_at = 102 * K
    gl, g_e, g_w = (sb(n, [P, 4, 8], F32, gate_at + 128 * i) for i, n in enumerate(("gl", "g_e", "g_w")))
    g_m, g_r = (sb(n, [P, 4], F32, gate_at + 384 + 32 * i) for i, n in enumerate(("g_m", "g_r")))
    g_rank = sb("g_rank", [P, 4, 8], F32, gate_at + 448)
    g_gt = sb("g_gt", [P, 4, 8, 8], F32, gate_at + 1024)
    g_eq = sb("g_eq", [P, 4, 8, 8], F32, gate_at + 2048)
    g_base = sb("g_base", [P, 4, 8], F32, gate_at + 704)
    w1q_hi, w1q_lo = (sb(f"w1q_{i}", [P, 2, NC, D], F32R, G_ + 6784 * j) for j, i in enumerate(("hi", "lo")))
    w1k_hi, w1k_lo = (sb(f"w1k_{i}", [P, 2, NC, P], F32R, G_ + 4096 + 6784 * j) for j, i in enumerate(("hi", "lo")))
    w1v_hi, w1v_lo = (sb(f"w1v_{i}", [P, NC, 64], F32R, G_ + 6144 + 6784 * j) for j, i in enumerate(("hi", "lo")))
    rope = sb("rope", [P, 2, T], F32, G_ + 14 * K)
    w1 = [[sb(f"w1_{n}{b}", [P, 3, 1024], F32R, H_ + 24 * K * b + 12 * K * j) for j, n in enumerate(("hi", "lo"))]
          for b in range(2)]
    raw1 = [stage, sb("stage2", [P, 3072], F32, D_)]
    wb1 = sb("wb1", [P, E1, T], F32, C_)
    x1_t = sb("x1_t", [P, NC, T], F32, 68 * K)
    wt1 = sb("wt1", [96, T], F32R, 76 * K)
    wst1 = sb("wst1", [P, NT, 96], F32R, 80 * K)
    y1_t = sb("y1_t", [P, NC, T], F32, 68 * K)
    m_s = sb("m_s", [P, 3, HALF], F32, 84 * K)
    m_sw = sb("m_sw", [P, 3, HALF], F32, 90 * K)
    m_g = sb("m_g", [P, 2, HALF], F32, 96 * K)
    m_ghi = sb("m_ghi", [P, 3, HALF], F32R, 100 * K)
    m_glo = sb("m_glo", [P, 3, HALF], F32R, 106 * K)
    r_at = 112 * K
    r_l, r_e, r_p, r_x, r_w = (sb(n, [P, NT, 8], F32, r_at + 256 * i)
                               for i, n in enumerate(("r_l", "r_e", "r_p", "r_x", "r_w")))
    r_m, r_s = (sb(n, [P, NT], F32, r_at + 1280 + 32 * i) for i, n in enumerate(("r_m", "r_s")))
    r_gt = sb("r_gt", [P, NT, 8, 8], F32, r_at + 2 * K)
    r_eq = sb("r_eq", [P, NT, 8, 8], F32, r_at + 4 * K)
    rw_sb = sb("rw_sb", [P, NC, 8], F32, r_at + 6 * K)
    PS = ctx.enter_context(nc.psum_tensor("PS", [P, 8, HALF], F32))

    sems = {}

    def sem(name):
        assert name not in sems, name
        sems[name] = ctx.enter_context(nc.semaphore(name))
        return sems[name]

    class Stage:

        @staticmethod
        def sync(sp):
            pass

        @staticmethod
        def gpsimd(pool):
            pass

        @staticmethod
        def scalar(act):
            pass

        @staticmethod
        def vector(dve):
            pass

        @staticmethod
        def tensor(pe):
            pass

    stages = []
    scr_q = nc.dram_tensor("scr_q", [2, PARTS, P, T], BF16).ap()
    scr_k = nc.dram_tensor("scr_k", [2, PARTS, P, T], BF16).ap()

    s_x = [sem(f"x_loaded{hf}") for hf in range(2)]
    s_lr = sem("adapters_loaded")
    s_id = sem("identity_loaded")
    s_tbl = sem("table_loaded")
    s_lora = sem("lora_product")
    s_cst = sem("consts_loaded")
    s_w0 = sem("attn0_weights_loaded")
    s_cst_b = sem("consts_ready")
    CONSTS, LOADED = 9, 16 * 11

    class Start(Stage):
        @staticmethod
        def sync(sp):
            sp.dma_start(lora[:], a["lora"].rearrange("k m r o -> r k m o")).then_inc(s_lr, 16)
            for hf in range(2):
                sp.dma_start(x_res[:, 4 * hf:4 * hf + 4, :],
                             a["x"].rearrange("(t p) d -> p t d", p=P)[:, 4 * hf:4 * hf + 4, :]).then_inc(s_x[hf], 16)
            sp.dma_start(wraw[:], a["w_attn0"].rearrange("m (c p) o -> p m c o", p=P)).then_inc(s_w0, 16)
            sp.dma_start(bqk[:], a["bqk"]).then_inc(s_cst, 16)
            sp.dma_start(bv_b[:], a["bvo"][0:1, :].broadcast_to([P, D])).then_inc(s_cst, 16)
            sp.dma_start(bo_b[:], a["bvo"][1:2, :].broadcast_to([96, D])).then_inc(s_cst, 16)
            sp.dma_start(mask_raw[:], a["masks"]).then_inc(s_cst, 16)
            sp.dma_start(tri[:], a["tri"]).then_inc(s_cst, 16)
            sp.dma_start(sel_raw[:], a["sel"]).then_inc(s_cst, 16)
            sp.dma_start(bst_raw[:], a["b_dn0"]).then_inc(s_cst, 16)
            sp.dma_start(b_up[:], a["b_up0"]).then_inc(s_cst, 16)
            sp.dma_start(b_sw[:], a["b_sw0"]).then_inc(s_cst, 16)
            sp.dma_start(b_sd[:], a["b_sd0"]).then_inc(s_cst, 16)
            sp.dma_start(bg_b[:], a["b_g0"].broadcast_to([P, ROUNDS, 8])).then_inc(s_cst, 16)

        @staticmethod
        def scalar(act):
            act.dma_start(ident[:], a["ident"]).then_inc(s_id, 16)
            act.wait_ge(s_cst_b, 1)
            act.activation(nmean[:, 0:1], mhalf[:, 0:1], ACT.Exp).then_inc(s_tbl, 1)

        @staticmethod
        def tensor(pe):
            pe.wait_ge(s_lr, 16)
            for m in range(4):
                for c in range(NC):
                    mm = pe.matmul(PS[:, 4 + m, D * c:D * c + D], lora[:, 1, m, P * c:P * c + P], lora[:, 0, m, :],
                                   start=True, stop=True)
                mm.then_inc(s_lora, 1)

        @staticmethod
        def gpsimd(pool):
            pool.memset(mhalf[:], -0.5).then_inc(s_cst_b, 1)

    stages.append(Start)

    POWER_STEPS = 4

    class Turned:
        t = sem("features_transposed")
        hi = sem("features_hi")
        lo = sem("features_lo")
        count = 0

        def __init__(self):
            self.base = 2 * NC * Turned.count
            Turned.count += 1

    class Norm:
        stat = sem("norm_stats")
        step = sem("norm_power")
        y = sem("norm_done_by_act")
        y_dve = sem("norm_done_by_dve")
        norms = act_tiles = dve_tiles = 0

        def __init__(self, act_tiles):
            self.stat0, self.pool0, self.y0 = 2 * NT * Norm.norms, 2 * POWER_STEPS * Norm.norms, Norm.act_tiles
            self.y0_dve = Norm.dve_tiles
            Norm.norms += 1
            Norm.act_tiles += act_tiles
            Norm.dve_tiles += NT - act_tiles

        def moments(self, dve, hf, src):
            for t in range(4 * hf, 4 * hf + 4):
                dve.bn_stats(stats[:, t, :], src(t)).then_inc(self.stat, 1)
            dve.wait_ge(self.stat, self.stat0 + 8 * hf + 4)
            for t in range(4 * hf, 4 * hf + 4):
                dve.bn_aggr(mv[:, t, :], stats[:, t, :]).then_inc(self.stat, 1)

        def power(self, pool, hf):
            ts = slice(4 * hf, 4 * hf + 4)
            steps = self.pool0 + POWER_STEPS * hf
            pool.wait_ge(self.stat, self.stat0 + 8 * hf + 8)
            pool.wait_ge(s_cst_b, 1)
            pool.wait_ge(s_tbl, 1)
            pool.tensor_scalar(rstd[:, ts], mv[:, ts, 1], EPS, None, ALU.add).then_inc(self.step, 1)
            pool.wait_ge(self.step, steps + 1)
            pool.tensor_tensor(rstd[:, ts], rstd[:, ts], mhalf[:, ts], ALU.pow).then_inc(self.step, 1)
            pool.tensor_scalar(nmean[:, ts], mv[:, ts, 0], -1.0, None, ALU.mult).then_inc(self.step, 1)
            pool.wait_ge(self.step, steps + 3)
            pool.tensor_tensor(nmean[:, ts], nmean[:, ts], rstd[:, ts], ALU.mult).then_inc(self.step, 1)

        def apply(self, act, hf, src, dst):
            act.wait_ge(self.step, self.pool0 + POWER_STEPS * (hf + 1))
            for t in range(4 * hf, 4 * hf + 4):
                act.activation(dst(t), src(t), ACT.Identity, bias=nmean[:, t:t + 1], scale=rstd[:, t:t + 1])\
                   .then_inc(self.y, 1)

        def apply_dve(self, dve, hf, src, dst):
            dve.wait_ge(self.step, self.pool0 + POWER_STEPS * hf + 2)
            for t in range(4 * hf, 4 * hf + 4):
                dve.tensor_scalar(dst(t), src(t), mv[:, t, 0:1], rstd[:, t:t + 1], ALU.subtract, ALU.mult)\
                   .then_inc(self.y_dve, 1)

    def norms(tag, work, src=None, wait_src=None, wait_x=None, transposed=True, keep=None,
              split_later=False):
        post = Norm(NT) if src else None
        pre = Norm(NT // 2) if transposed else None
        s_new = sem(tag + "_x")
        turned = Turned() if transposed else None
        s_keep = sem(tag + "_kept") if keep else None

        class Norms(Stage):
            x, features, kept = s_new, turned, s_keep

            @staticmethod
            def vector(dve):
                if src:
                    for hf in range(2):
                        wait_src(dve, hf)
                        post.moments(dve, hf, src)
                for hf in range(2):
                    if src:
                        for t in range(4 * hf, 4 * hf + 4):
                            dve.wait_ge(post.y, post.y0 + t + 1)
                            dve.tensor_tensor(x_res[:, t, :], x_res[:, t, :], work[:, t, :], ALU.add).then_inc(s_new, 1)
                        dve.wait_ge(s_new, 4 * hf + 4)
                    else:
                        wait_x(dve, hf)
                    if transposed:
                        pre.moments(dve, hf, lambda t: x_res[:, t, :])
                if transposed:
                    pre.apply_dve(dve, 1, lambda t: x_res[:, t, :], lambda t: work[:, t, :])
                    if not split_later:
                        Norms.split(dve)

            @staticmethod
            def hi_one(act, k):
                hf, c = divmod(k, 2)
                act.wait_ge(turned.t, turned.base + k + 1)
                act.activation(xhi[:, c, HALF * hf:HALF * hf + HALF], PS[:, k, :], ACT.Copy).then_inc(turned.hi, 1)

            @staticmethod
            def split(dve):
                for k in range(2 * NC):
                    Norms.split_one(dve, k)

            @staticmethod
            def split_one(dve, k):
                hf, c = divmod(k, 2)
                dve.wait_ge(turned.hi, turned.base + k + 1)
                dve.tensor_tensor(xlo[:, c, HALF * hf:HALF * hf + HALF], PS[:, k, :],
                                  xhi[:, c, HALF * hf:HALF * hf + HALF].bitcast(F32), ALU.subtract)\
                   .then_inc(turned.lo, 1)

            @staticmethod
            def gpsimd(pool):
                for n in (post, pre):
                    if n:
                        for hf in range(2):
                            n.power(pool, hf)

            @staticmethod
            def tensor(pe):
                if transposed:
                    pe.wait_ge(s_id, 16)
                    for hf in range(2):
                        if hf == 0:
                            pe.wait_ge(pre.y, pre.y0 + 4)
                        else:
                            pe.wait_ge(pre.y_dve, pre.y0_dve + 4)
                        for c in range(NC):
                            for i in range(4):
                                m = pe.transpose(PS[:, 2 * hf + c, P * i:P * i + P],
                                                 work[:, 4 * hf + i, P * c:P * c + P], ident[:])
                            m.then_inc(turned.t, 1)

            @staticmethod
            def scalar(act):
                if src:
                    for hf in range(2):
                        post.apply(act, hf, src, lambda t: work[:, t, :])
                if transposed:
                    if wait_x:
                        wait_x(act, 0)
                    pre.apply(act, 0, lambda t: x_res[:, t, :], lambda t: work[:, t, :])
                    if split_later:
                        return
                    for hf in range(2):
                        for k in (2 * hf, 2 * hf + 1):
                            Norms.hi_one(act, k)
                        if keep:
                            for k in (2 * hf, 2 * hf + 1):
                                c = k % 2
                                act.wait_ge(turned.lo, turned.base + k + 1)
                                act.activation(keep[:, c, HALF * hf:HALF * hf + HALF], PS[:, k, :], ACT.Copy)\
                                   .then_inc(s_keep, 1)
        return Norms

    def bank_tile(t):
        return PS[:, 4 + t // 2, D * (t % 2):D * (t % 2) + D]

    xn = sb("xn", [P, NT, D], F32, G_ + 12 * K)
    pre0 = norms("pre0", xn, wait_x=lambda eng, hf: eng.wait_ge(s_x[hf], 16), split_later=True)
    s_weff = sem("w_eff")
    s_whi = sem("w_eff_hi")
    s_wlo = sem("w_eff_lo")

    def w0(m, lo):
        if m == 3:
            return wo_lo if lo else wo_hi
        return (wqkv_lo if lo else wqkv_hi)[:, m, :, :]

    class Weights0(Stage):

        @staticmethod
        def vector(dve):
            dve.wait_ge(s_w0, 16)
            for m in range(4):
                dve.wait_ge(s_lora, m + 1)
                dve.scalar_tensor_tensor(weff[:, m, :, :], PS[:, 4 + m, :].rearrange("p (c o) -> p c o", c=NC), 0.5,
                                         wraw[:, m, :, :], ALU.mult, ALU.add).then_inc(s_weff, 1)
            for m in range(4):
                dve.wait_ge(s_whi, m + 1)
                dve.tensor_tensor(w0(m, 1)[:], weff[:, m, :, :], w0(m, 0)[:].bitcast(F32), ALU.subtract)\
                   .then_inc(s_wlo, 1)
                pre0.split_one(dve, m)

        @staticmethod
        def scalar(act):
            for m in range(4):
                act.wait_ge(s_weff, m + 1)
                act.activation(w0(m, 0)[:], weff[:, m, :, :], ACT.Copy).then_inc(s_whi, 1)
                pre0.hi_one(act, m)

    class Constants(Stage):
        @staticmethod
        def gpsimd(pool):
            pool.wait_ge(s_cst_b, 1)
            pool.wait_ge(Norm.step, 2 * POWER_STEPS)
            pool.memset(vaug[:], 1.0).then_inc(s_cst_b, 1)
            pool.wait_ge(s_cst_b, 2)
            pool.memset(ka[0][96:99, :, :], 1.0).then_inc(s_cst_b, 1)
            pool.wait_ge(s_cst_b, 3)
            pool.memset(ka[1][96:99, :, :], 1.0).then_inc(s_cst_b, 1)
            pool.wait_ge(s_id, 16)
            pool.wait_ge(s_cst, LOADED)
            pool.wait_ge(s_cst_b, 4)
            pool.tensor_copy(ident_b[:], ident[:]).then_inc(s_cst_b, 1)
            pool.wait_ge(s_cst_b, 5)
            pool.tensor_copy(mask_b[:], mask_raw[:]).then_inc(s_cst_b, 1)
            pool.wait_ge(s_cst_b, 6)
            pool.tensor_copy(sel[:], sel_raw[:]).then_inc(s_cst_b, 1)
            pool.wait_ge(s_cst_b, 7)
            pool.tensor_copy(bo_st[:], bo_b[:]).then_inc(s_cst_b, 1)
            pool.wait_ge(s_cst_b, 8)
            pool.tensor_tensor(bo_st[32:64, :], bo_b[32:64, :], bo_st[32:64, :].bitcast(F32), ALU.subtract)\
                .then_inc(s_cst_b, 1)

    stages.append(pre0)
    stages.append(Weights0)
    stages.append(Constants)

    def product(pe, ps, w_hi, w_lo, x_hi, x_lo, chunks, start=True, stop=True):
        n = 3 * chunks
        k = 0
        for c in range(chunks):
            for w, x in ((w_hi, x_hi), (w_lo, x_hi), (w_hi, x_lo)):
                m = pe.matmul(ps, w(c), x(c), start=start and k == 0, stop=stop and k == n - 1)
                k += 1
        return m

    def split_parts(tag, units):
        s_f = sem(tag + "_f32")
        s_p1, s_d, s_p2, s_p3 = (sem(tag + x) for x in ("_part1", "_rest", "_part2", "_part3"))

        class Split:
            f, p1, d, p2, p3 = s_f, s_p1, s_d, s_p2, s_p3

            @staticmethod
            def free(eng, n):
                if n >= 2:
                    eng.wait_ge(s_p1, n - 1)
                    eng.wait_ge(s_d, n - 1)

            @staticmethod
            def act_first(act, n):
                dst, hf = units[n]
                act.wait_ge(s_f, n + 1)
                act.activation(dst[:, 0, HALF * hf:HALF * hf + HALF], qf[:, n % 2, :], ACT.Copy).then_inc(s_p1, 1)

            @staticmethod
            def act_second(act, n):
                dst, hf = units[n]
                act.wait_ge(s_d, n + 1)
                act.activation(dst[:, 1, HALF * hf:HALF * hf + HALF], qd[:, n % 2, :], ACT.Copy).then_inc(s_p2, 1)

            @staticmethod
            def dve_free(dve, n):
                dve.wait_ge(s_p1, n + 1)
                if n >= 2:
                    dve.wait_ge(s_p2, n - 1)
                    dve.wait_ge(s_p3, n - 1)

            @staticmethod
            def dve_first(dve, n):
                dst, hf = units[n]
                Split.dve_free(dve, n)
                dve.tensor_tensor(qd[:, n % 2, :], qf[:, n % 2, :], dst[:, 0, HALF * hf:HALF * hf + HALF],
                                  ALU.subtract).then_inc(s_d, 1)

            @staticmethod
            def dve_second(dve, n):
                dst, hf = units[n]
                dve.wait_ge(s_p2, n + 1)
                dve.wait_ge(s_d, n + 1)
                dve.tensor_tensor(dst[:, 2, HALF * hf:HALF * hf + HALF], qd[:, n % 2, :],
                                  dst[:, 1, HALF * hf:HALF * hf + HALF], ALU.subtract).then_inc(s_p3, 1)
        return Split

    units0 = [(op, m, hf) for m in range(2) for op in range(2) for hf in range(2)]
    split0 = split_parts("qk0", [(parts[2 * m + op], hf) for op, m, hf in units0])
    s_qk0 = sem("qk0_product")
    s_v0 = sem("v0_product")
    s_vaug0 = sem("v0_ready")
    s_scr0 = [sem(f"qk0_in_scratch_{n}") for n in ("q", "k", "rest")]

    def store_parts0(sp, m):
        for op, scr in enumerate((scr_q, scr_k)):
            sp.wait_ge(split0.p3, 4 * m + 2 * op + 2)
            sp.dma_start(scr[m].rearrange("s p t -> p s t"), parts[2 * m + op][:])\
              .then_inc(s_scr0[2 if m else op], 16)

    class Project0(Stage):
        @staticmethod
        def tensor(pe):
            for n, (op, m, hf) in enumerate(units0):
                pe.wait_ge(s_wlo, op + 1)
                pe.wait_ge(pre0.features.lo, pre0.features.base + 2 * hf + 2)
                if n >= 2:
                    pe.wait_ge(split0.d, n - 1)
                h = slice(HALF * hf, HALF * hf + HALF)
                product(pe, PS[:, 4 + n % 2, :],
                        lambda c: wqkv_hi[:, op, c, P * m:P * m + P], lambda c: wqkv_lo[:, op, c, P * m:P * m + P],
                        lambda c: xhi[:, c, h], lambda c: xlo[:, c, h], NC).then_inc(s_qk0, 1)
            pe.wait_ge(s_wlo, 3)
            for n in range(NT):
                t = slice(P * n, P * n + P)
                if n >= 4:
                    pe.wait_ge(s_vaug0, n - 3)
                product(pe, PS[:, (6, 7, 2, 3)[n % 4], 0:D], lambda c: xhi[:, c, t], lambda c: xlo[:, c, t],
                        lambda c: wqkv_hi[:, 2, c, :], lambda c: wqkv_lo[:, 2, c, :], NC).then_inc(s_v0, 1)

        @staticmethod
        def scalar(act):
            act.wait_ge(s_cst, LOADED)
            for n, (op, m, hf) in enumerate(units0):
                act.wait_ge(s_qk0, n + 1)
                act.activation(parts[2 * m + op][:, 0, HALF * hf:HALF * hf + HALF], PS[:, 4 + n % 2, :], ACT.Identity,
                               bias=bqk[:, op, m:m + 1]).then_inc(split0.p1, 1)
                if n >= 1:
                    split0.act_second(act, n - 1)
            split0.act_second(act, len(units0) - 1)

        @staticmethod
        def vector(dve):
            for n, (op, m, hf) in enumerate(units0):
                split0.dve_free(dve, n)
                dve.scalar_tensor_tensor(qd[:, n % 2, :], PS[:, 4 + n % 2, :], bqk[:, op, m:m + 1],
                                         parts[2 * m + op][:, 0, HALF * hf:HALF * hf + HALF], ALU.add, ALU.subtract)\
                   .then_inc(split0.d, 1)
                if n >= 1:
                    split0.dve_second(dve, n - 1)
            split0.dve_second(dve, len(units0) - 1)
            dve.wait_ge(s_cst_b, CONSTS)
            for n in range(NT):
                dve.wait_ge(s_v0, n + 1)
                dve.tensor_tensor(vaug[:, n, 0:HEADS * VW].rearrange("p (h w) -> p h w", w=VW)[:, :, 0:HD],
                                  PS[:, (6, 7, 2, 3)[n % 4], 0:D].rearrange("p (h w) -> p h w", w=HD),
                                  bv_b[:].rearrange("p (h w) -> p h w", w=HD), ALU.add).then_inc(s_vaug0, 1)

        @staticmethod
        def sync(sp):
            store_parts0(sp, 0)

    stages.append(Project0)

    def attention(tag, causal, s_scr, rest_count, v_ready, kv_heads, store_rest, early, extra_pool=None):
        units = [(g, qh) for g in range(GROUPS) for qh in range(2)]
        steps, tstart = [], []
        for u, (g, qh) in enumerate(units):
            tstart.append(len(steps))
            for kt in range(4 * (qh + 1) if causal else NT):
                steps.append((u, kt, max(0, P * kt - HALF * qh) if causal else 0))
        tstart.append(len(steps))
        NS = len(steps)
        tiles, send = [], []
        for u, (g, qh) in enumerate(units):
            for hl in range(GH):
                for qt in range(4):
                    keys = P * (4 * qh + qt + 1) if causal else T
                    for kh in range(-(-keys // HALF)):
                        tiles.append((u, hl, qt, kh, min(HALF, keys - HALF * kh)))
            send.append(len(tiles))
        assert len(tiles) == 4 * NS
        n_kh = [1 if causal and qh == 0 else 2 for g, qh in units]
        s_s = sem(tag + "_scores")
        s_max = sem(tag + "_tile_max")
        s_nm = sem(tag + "_negated_max")
        NM = 4
        s_neg = sem(tag + "_unit_max")
        s_nmT = sem(tag + "_max_transposed")
        s_nmE = sem(tag + "_max_evacuated")
        s_nmR = [sem(f"{tag}_max_rows{i}") for i in range(2)]
        s_T = sem(tag + "_scoresT")
        s_e = sem(tag + "_exp")
        s_pv = sem(tag + "_pv")
        s_oE = sem(tag + "_out_evacuated")
        s_oT = sem(tag + "_out_transposed")
        s_rd = sem(tag + "_reciprocal")
        s_at = sem(tag + "_attn")
        k_once = kv_heads == GROUPS
        qbuf = qa + [qa2] if k_once else qa
        NB = len(qbuf)
        s_k = [sem(f"{tag}_keys{i}") for i in range(1 if k_once else 2)]
        s_q = [[sem(f"{tag}_queries{i}_{qh}") for qh in range(2)] for i in range(NB)]
        PER_LOAD = SLOTS * 16

        def operands(eng, g, qh):
            if k_once:
                eng.wait_ge(s_k[0], PER_LOAD)
            else:
                eng.wait_ge(s_k[g % 2], PER_LOAD * (g // 2 + 1))
            eng.wait_ge(s_q[g % NB][qh], PER_LOAD * (g // NB + 1))

        def load_q(eng, g, qh):
            m, off = g // 2, 64 * (g % 2)
            for i in range(SLOTS):
                eng.dma_start(qbuf[g % NB][HD * i:HD * i + HD, qh, :, :],
                              scr_q[m, Q_SLOT[i], off:off + 64, HALF * qh:HALF * qh + HALF]
                              .rearrange("(h d) t -> d h t", h=GH)).then_inc(s_q[g % NB][qh], 16)

        def load_k(eng, g):
            m, off = g // 2, 64 * (g % 2)
            if not k_once or g == 0:
                for i in range(SLOTS):
                    eng.dma_start(ka[g % 2][HD * i:HD * i + HD, :, :],
                                  scr_k[m, K_SLOT[i], off:off + 64, :].rearrange("(h d) t -> d h t", h=GH))\
                       .then_inc(s_k[g % 2], 16)

        def kop(g, hl):
            return (ka[0], g) if k_once else (ka[g % 2], hl)

        def s_banks(i):
            return 6 if i < send[0] + early else 2

        def tiles_before(s):
            return min(len(tiles), 4 * (s + LEAD))

        class Att(Stage):
            attn_ready = s_at

            @staticmethod
            def sync(sp):
                sp.wait_ge(s_scr[0], 16)
                load_q(sp, 0, 0)
                sp.wait_ge(s_scr[1], 16)
                load_k(sp, 0)
                load_q(sp, 0, 1)
                store_rest(sp, 1)
                load_k(sp, 1)
                load_q(sp, 1, 0)
                for v in range(len(units)):
                    g, qh = units[v]
                    sp.wait_ge(s_nmE, v + 1)
                    for p in range(PARTS):
                        sp.dma_start(qbuf[g % NB][KS + p:KS + p + 1, qh, :, :].rearrange("p h c -> p (h c)")
                                     .rearrange("p (r c) -> p r c", c=P),
                                     nmt[16 * p:16 * p + 16, v % 2, :]).then_inc(s_nmR[v % 2], 16)
                    if v == 0:
                        load_q(sp, 1, 1)
                        if NB == 3:
                            sp.wait_ge(s_scr[2], rest_count)
                            load_q(sp, 2, 0)
                            load_q(sp, 2, 1)
                    if qh == 0 and 1 <= g <= GROUPS - NB:
                        sp.wait_ge(s_scr[2], rest_count)
                        sp.wait_ge(s_T, 2 * tstart[2 * g])
                        load_k(sp, g + NB - 1)
                        load_q(sp, g + NB - 1, 0)
                        load_q(sp, g + NB - 1, 1)

            @staticmethod
            def gpsimd(pool):
                for v in range(len(units)):
                    b = v % 2
                    pool.wait_ge(s_neg, v + 1)
                    if v >= 2:
                        pool.wait_ge(s_nmT, v - 1)
                    k = NM * v
                    pool.tensor_copy(nmp[:, b, 0, :], nmd[:, b, :]).then_inc(s_nm, 1)
                    pool.wait_ge(s_nm, k + 1)
                    pool.tensor_tensor(nmf[:, b, :], nmd[:, b, :], nmp[:, b, 0, :], ALU.subtract).then_inc(s_nm, 1)
                    pool.wait_ge(s_nm, k + 2)
                    pool.tensor_copy(nmp[:, b, 1, :], nmf[:, b, :]).then_inc(s_nm, 1)
                    pool.wait_ge(s_nm, k + 3)
                    pool.tensor_tensor(nmp[:, b, 2, :], nmf[:, b, :], nmp[:, b, 1, :], ALU.subtract).then_inc(s_nm, 1)
                    if extra_pool:
                        extra_pool(pool, v)

            @staticmethod
            def tensor(pe):
                misc = [None]

                def misc_free():
                    if misc[0]:
                        pe.wait_ge(*misc[0])

                def s_tile(i):
                    u, hl, qt, kh, w = tiles[i]
                    g, qh = units[u]
                    if i == 0 or tiles[i - 1][0] != u:
                        operands(pe, g, qh)
                    if i >= s_banks(i):
                        pe.wait_ge(s_max, i + 1 - s_banks(i))
                    kb, kx = kop(g, hl)
                    diag = causal and HALF * kh + w == P * (4 * qh + qt + 1)
                    m = pe.matmul(PS[:, i % s_banks(i), 0:w], qbuf[g % NB][0:KS, qh, hl, P * qt:P * qt + P],
                                  kb[0:KS, kx, HALF * kh:HALF * kh + w], start=True, stop=not diag)
                    if diag:
                        m = pe.matmul(PS[:, i % s_banks(i), w - P:w], ident_b[:], mask_b[:, 0, :], start=False, stop=True)
                    m.then_inc(s_s, 1)

                def max_rows(v):
                    misc_free()
                    pe.wait_ge(s_nm, NM * v + NM)
                    pe.transpose(PS[0:48, 7, 0:64].bitcast(BF16), nmp[:, v % 2, :, :].rearrange("p s r -> p (s r)"),
                                 ident_b[:]).then_inc(s_nmT, 1)
                    misc[0] = (s_nmE, v + 1)

                def out_tiles(v):
                    misc_free()
                    pe.wait_ge(s_oE, v + 1)
                    for i in range(4):
                        m = pe.transpose(PS[:, 7, P * i:P * i + P], o_t[:, v % 2, P * i:P * i + P], ident[:])
                    m.then_inc(s_oT, 1)
                    misc[0] = (s_at, v + 1)

                def pv(s):
                    u, kt, q0 = steps[s]
                    g, qh = units[u]
                    pe.wait_ge(s_e, 2 * s + 2)
                    if kt == 0 and u >= 1:
                        pe.wait_ge(s_oE, u)
                    last = s == tstart[u + 1] - 1
                    for hl in range(GH):
                        w = VW * (g if k_once else GH * g + hl)
                        m = pe.matmul(PS[32 * hl:32 * hl + 32, 6, q0:HALF], vaug[:, kt, w:w + 32],
                                      pt[:, (2 * s + hl // 2) % 6, hl % 2, q0:HALF], start=kt == 0, stop=last)
                    m.then_inc(s_pv, 1)

                pe.wait_ge(s_cst_b, CONSTS)
                v_ready(pe)
                first = send[0]
                for i in range(first):
                    s_tile(i)
                for i in range(first, first + early):
                    if i == first + AHEAD:
                        max_rows(0)
                    s_tile(i)
                done = first + early
                pe.wait_ge(s_max, done)
                for s in range(NS + 4):
                    for v in range(len(units)):
                        if v >= 1 and s == max(1, tstart[v] - 3):
                            while done < send[v]:
                                s_tile(done)
                                done += 1
                            max_rows(v)
                        if s == tstart[v + 1] + 2:
                            out_tiles(v)
                    if s < NS:
                        u, kt, q0 = steps[s]
                        g, qh = units[u]
                        if s == tstart[u]:
                            pe.wait_ge(s_nmR[u % 2], 48 * (u // 2 + 1))
                        for pr in range(2):
                            pair = 2 * s + pr
                            if pair >= 2:
                                pe.wait_ge(s_e, pair - 1)
                            for hl in (2 * pr, 2 * pr + 1):
                                kb, kx = kop(g, hl)
                                diag = causal and P * kt >= HALF * qh
                                m = pe.matmul(PS[:, 2 + hl, q0:HALF], kb[0:KM, kx, P * kt:P * kt + P],
                                              qbuf[g % NB][0:KM, qh, hl, q0:HALF], start=True, stop=not diag)
                                if diag:
                                    m = pe.matmul(PS[:, 2 + hl, q0:q0 + P], ident_b[:], mask_b[:, 1, :],
                                                  start=False, stop=True)
                            m.then_inc(s_T, 1)
                            for _ in range(1):
                                if done < tiles_before(s + 1):
                                    s_tile(done)
                                    done += 1
                    if 1 <= s <= NS:
                        pv(s - 1)
                    if s < NS:
                        while done < tiles_before(s + 1):
                            s_tile(done)
                            done += 1
                    assert s < NS or done == len(tiles)

            @staticmethod
            def scalar(act):
                def max_evac(v):
                    act.wait_ge(s_nmT, v + 1)
                    if v >= 2:
                        act.wait_ge(s_nmR[v % 2], 48 * (v // 2))
                    act.activation(nmt[:, v % 2, :], PS[0:48, 7, 0:64].bitcast(BF16), ACT.Copy).then_inc(s_nmE, 1)

                max_evac(0)
                for s in range(NS + 1):
                    for v in range(1, len(units)):
                        if s == max(1, tstart[v] - 3):
                            max_evac(v)
                    if s < NS:
                        q0 = steps[s][2]
                        for pr in range(2):
                            pair = 2 * s + pr
                            act.wait_ge(s_T, pair + 1)
                            if pair >= 6:
                                act.wait_ge(s_pv, (pair - 6) // 2 + 1)
                            act.activation(pt[:, pair % 6, :, q0:HALF], PS[:, 2 + 2 * pr:4 + 2 * pr, q0:HALF],
                                           ACT.Exp, scale=0.25).then_inc(s_e, 1)
                    for v in range(len(units)):
                        if s == tstart[v + 1]:
                            act.wait_ge(s_pv, s)
                            if v >= 2:
                                act.wait_ge(s_oT, v - 1)
                            act.activation(o_t[:, v % 2, :], PS[:, 6, :], ACT.Copy).then_inc(s_oE, 1)

            @staticmethod
            def vector(dve):
                def normalise(v):
                    g, qh = units[v]
                    dve.wait_ge(s_oT, v + 1)
                    if v >= 2:
                        dve.wait_ge(s_at, v - 1)
                    o = PS[:, 7, :].rearrange("p (t h w) -> p t h w", t=4, w=32)
                    dve.reciprocal(rden[:, v % 2, :, :], o[:, :, :, HD]).then_inc(s_rd, 1)
                    dve.wait_ge(s_rd, v + 1)
                    dve.tensor_tensor(attn[:, 4 * qh:4 * qh + 4, GH * HD * g:GH * HD * (g + 1)]
                                      .rearrange("p t (h w) -> p t h w", w=HD), o[:, :, :, 0:HD],
                                      rden[:, v % 2, :, :].unsqueeze(3).broadcast_to([P, 4, GH, HD]), ALU.mult).then_inc(s_at, 1)

                todo = list(range(len(units)))
                for i in range(len(tiles)):
                    u, hl, qt, kh, w = tiles[i]
                    while todo and tiles_before(tstart[todo[0] + 1] + 3) <= min(i, len(tiles) - 1):
                        normalise(todo.pop(0))
                    dve.wait_ge(s_s, i + 1)
                    if hl == 0 and qt == 0 and kh == 0 and u >= 2:
                        dve.wait_ge(s_neg, u - 1)
                    dve.tensor_reduce(mx[:, u % 2, 4 * hl + qt, kh:kh + 1], PS[:, i % s_banks(i), 0:w], AX.X, ALU.max)\
                       .then_inc(s_max, 1)
                    if i + 1 == send[u]:
                        dve.wait_ge(s_max, i + 1)
                        if u >= 2:
                            dve.wait_ge(s_nm, NM * (u - 2) + 2)
                        dve.tensor_reduce(nmd[:, u % 2, :], mx[:, u % 2, :, 0:n_kh[u]], AX.X, ALU.max, negate=True)\
                           .then_inc(s_neg, 1)
                while todo:
                    normalise(todo.pop(0))
        return Att


    def out_projection(tag, att, wo_ready, bias):
        turned = Turned()
        s_o = sem(tag + "_product")

        class Out(Stage):
            ready = s_o

            @staticmethod
            def tensor(pe):
                for hf in range(2):
                    pe.wait_ge(att.attn_ready, 7 + hf)
                    for c in range(NC):
                        for i in range(4):
                            m = pe.transpose(PS[:, 2 * hf + c, P * i:P * i + P],
                                             attn[:, 4 * hf + i, P * c:P * c + P], ident[:])
                        m.then_inc(turned.t, 1)
                wo_ready(pe)
                for n in range(NT):
                    t = slice(P * n, P * n + P)
                    pe.wait_ge(turned.lo, turned.base + 2 * (n // 4) + 2)
                    m = product(pe, bank_tile(n), lambda c: xhi[:, c, t], lambda c: xlo[:, c, t],
                                lambda c: wo_hi[:, c, :], lambda c: wo_lo[:, c, :], NC, stop=bias is None)
                    if bias is not None:
                        m = pe.matmul(bank_tile(n), sel[:, 0, :], bias[:], start=False, stop=True)
                    m.then_inc(s_o, 1)

            @staticmethod
            def scalar(act):
                for k in range(4):
                    hf, c = divmod(k, 2)
                    act.wait_ge(turned.t, turned.base + k + 1)
                    act.activation(xhi[:, c, HALF * hf:HALF * hf + HALF], PS[:, k, :], ACT.Copy).then_inc(turned.hi, 1)

            @staticmethod
            def vector(dve):
                for k in range(4):
                    hf, c = divmod(k, 2)
                    dve.wait_ge(turned.hi, turned.base + k + 1)
                    dve.tensor_tensor(xlo[:, c, HALF * hf:HALF * hf + HALF], PS[:, k, :],
                                      xhi[:, c, HALF * hf:HALF * hf + HALF].bitcast(F32), ALU.subtract).then_inc(turned.lo, 1)
        return Out

    s_wf_ld = [sem(f"ffn0_weights_loaded{i}") for i in range(2)]
    s_wf = sem("ffn0_weights_split")
    up_raw = stage[:, 0:2048]
    CH = 512

    def flat(t):
        v = t[:]
        while v.ndim > 2:
            v = v.rearrange("p a b -> p (a b)") if v.ndim == 3 else v.rearrange("p a b c -> p (a b c)")
        return v

    f0_chunks = []
    for k in range(4):
        f0_chunks.append((0, stage[:, CH * k:CH * k + CH], flat(w_up_hi)[:, CH * k:CH * k + CH],
                          flat(w_up_lo)[:, CH * k:CH * k + CH]))
    for k in range(2):
        f0_chunks.append((1, stage[:, CH * k:CH * k + CH], flat(w_sw_hi)[:, CH * k:CH * k + CH],
                          flat(w_sw_lo)[:, CH * k:CH * k + CH]))
    for k in range(4):
        f0_chunks.append((1, stage[:, 1024 + CH * k:1024 + CH * k + CH], flat(w_dn_hi)[:, CH * k:CH * k + CH],
                          flat(w_dn_lo)[:, CH * k:CH * k + CH]))

    def split_f0(pool, v):
        if v == 0:
            pool.dma_start(stage[:, 0:2048], a["w_f0"][:, 0:2048]).then_inc(s_wf_ld[0], 16)
            return
        for n in range(2 * (v - 1), min(2 * v, len(f0_chunks))):
            piece, raw, hi, lo = f0_chunks[n]
            if n == 0:
                pool.wait_ge(s_wlo, 4)
            if n in (0, 4):
                pool.wait_ge(s_wf_ld[piece], 16)
            pool.tensor_copy(hi, raw).then_inc(s_wf, 1)
            pool.wait_ge(s_wf, 2 * n + 1)
            pool.tensor_tensor(lo, raw, hi.bitcast(F32), ALU.subtract).then_inc(s_wf, 1)
            pool.wait_ge(s_wf, 2 * n + 2)
            if n == 3:
                pool.dma_start(stage[:], a["w_f0"][:, 2048:5120]).then_inc(s_wf_ld[1], 16)

    F0_SPLIT = 20
    att0 = attention("att0", False, s_scr0, 32, lambda pe: pe.wait_ge(s_vaug0, NT), HEADS, store_parts0,
                     EARLY0, split_f0)
    stages.append(att0)
    out0 = out_projection("out0", att0, lambda pe: pe.wait_ge(s_wlo, 4), bo_st)
    stages.append(out0)
    work0 = sb("work0", [P, NT, D], F32, 70 * K)
    post0 = pre_f0 = norms("to_f0", work0, bank_tile, lambda dve, hf: dve.wait_ge(out0.ready, 4 * hf + 4), keep=res_t)
    stages.append(post0)

    def stands_before(dve, step, logit, gt, eq, n):
        lj = logit[:].unsqueeze(2).broadcast_to([P, n, 8, 8])
        li = logit[:].unsqueeze(3).broadcast_to([P, n, 8, 8])
        dve.tensor_tensor(gt[:], lj, li, ALU.is_gt).then_inc(step.sem, 1)
        dve.tensor_tensor(eq[:], lj, li, ALU.is_equal).then_inc(step.sem, 1)
        step.wait(dve, 2)
        dve.tensor_tensor(eq[:], eq[:], tri[:].unsqueeze(1).broadcast_to([P, n, 8, 8]), ALU.mult).then_inc(step.sem, 1)
        step.wait(dve, 1)
        dve.tensor_tensor(gt[:], gt[:], eq[:], ALU.add).then_inc(step.sem, 1)
        step.wait(dve, 1)

    class Steps:

        def __init__(self, s, at=0):
            self.sem, self.at = s, at

        def wait(self, eng, k):
            self.at += k
            eng.wait_ge(self.sem, self.at)

    def stack_weights(dve, step, w, st):
        dve.tensor_copy(st[:, :, 0:8], w[:]).then_inc(step.sem, 1)
        step.wait(dve, 1)
        dve.tensor_tensor(st[:, :, 32:40], w[:], st[:, :, 0:8].bitcast(F32), ALU.subtract).then_inc(step.sem, 1)
        dve.tensor_copy(st[:, :, 64:72], st[:, :, 0:8].bitcast(F32)).then_inc(step.sem, 1)
        step.wait(dve, 2)

    NQ = 2 * ROUNDS
    NK0 = NQ * N0
    s_up = sem("f0_up")
    s_hhi = sem("f0_h_hi")
    s_hlo = sem("f0_h_lo")
    s_sg = sem("f0_inner")
    s_si = sem("f0_silu")
    s_sp = sem("f0_silu_weighted")
    s_g = sem("f0_g")
    s_ghi = sem("f0_g_hi")
    s_glo = sem("f0_g_lo")
    s_dn = sem("f0_down")
    s_acc = sem("f0_sum")
    s_xh = sem("f0_x_hi")
    s_xl = sem("f0_x_lo")
    s_gm = sem("f0_gate_logits")
    s_gs = sem("f0_gate_step")
    GSTEPS = 15
    s_gb = sem("f0_base_ready")
    s_gx = sem("f0_gate_exp")
    s_gT = sem("f0_gate_transposed")
    s_gE = sem("f0_gate_evacuated")
    s_wbm = sem("f0_weight_broadcast")
    s_wbe = sem("f0_weight_ready")
    s_f0c = sem("f0_constants")
    s_wgl = sem("f0_gate_weights_loaded")

    FLAG, ULAG = 3, 4
    def gate_slot(q):
        return max(0, N0 * q - 1)

    def gate_part_slot(q, part):
        return gate_slot(q) + (part if part < 2 else 3 if q == 0 else 4)

    def gate_exp_slot(q, i):
        return gate_slot(q) + 1 + (0 if q == 0 else min(i, 2))

    def rows_slot(q):
        return gate_part_slot(q, 2) + 1

    def spread_slot(q, e):
        return rows_slot(q) + (e + 1) // 2

    def sum_slot(k):
        q, r = divmod(k - ULAG - N0 + 1, N0)
        return q if r == 0 and 0 <= q < NQ else None

    class Ffn0(Stage):
        @staticmethod
        def sync(sp):
            sp.dma_start(wg_sb[:], a["w_g0"]).then_inc(s_wgl, 16)

        @staticmethod
        def tensor(pe):
            def gate(q):
                r, hf = divmod(q, 2)
                if q == 0:
                    pe.wait_ge(s_wgl, 16)
                if q < 2:
                    pe.wait_ge(pre_f0.kept, 2 * q + 2)
                elif q >= 2:
                    pe.wait_ge(s_acc, 2 * (q - 1))
                if q >= 1:
                    pe.wait_ge(s_wbe, E0 * q)
                for i in range(4):
                    for c in range(NC):
                        m = pe.matmul(PS[:, 7, 8 * i:8 * i + 8], (xc_t if r else res_t)[:, c, HALF * hf + P * i:HALF * hf + P * i + P],
                                      wg_sb[:, r, c, :], start=c == 0, stop=c == NC - 1)
                m.then_inc(s_gm, 1)

            def rows(q):
                pe.wait_ge(s_gs, GSTEPS * (q + 1))
                for i in range(4):
                    m = pe.transpose(PS[0:96, 7, P * i:P * i + P], wst[:, i, :].bitcast(F32), ident[:])
                m.then_inc(s_gT, 1)

            def spread(q, e):
                n = E0 * q + e
                pe.wait_ge(s_gE, q + 1)
                if e:
                    pe.wait_ge(s_wbe, n)
                pe.matmul(PS[:, 7, :], sel[:, e, :], wt0[:, q % 2, :], start=True, stop=True).then_inc(s_wbm, 1)

            def up(k):
                q, n = divmod(k, N0)
                hf = q % 2
                if n == 0:
                    if q < 2:
                        pe.wait_ge(pre_f0.features.lo, pre_f0.features.base + 2 * hf + 2)
                    else:
                        pe.wait_ge(s_xl, 2 * (q - 1))
                if k >= 4:
                    pe.wait_ge(s_g, k - 3)
                else:
                    pe.wait_ge(pre_f0.kept, k + 1)
                h = slice(HALF * hf, HALF * hf + HALF)
                product(pe, PS[:, k % 4, :], lambda c: w_up_hi[:, n, c, :], lambda c: w_up_lo[:, n, c, :],
                        lambda c: xhi[:, c, h], lambda c: xlo[:, c, h], NC).then_inc(s_up, 1)

            def inner(k):
                n = k % N0
                pe.wait_ge(s_hlo, k + 1)
                if k >= 1:
                    pe.wait_ge(s_si, k)
                product(pe, PS[:, 4, :], lambda c: w_sw_hi[:, n, :], lambda c: w_sw_lo[:, n, :],
                        lambda c: h_hi[:, k % 2, :], lambda c: h_lo[:, k % 2, :], 1).then_inc(s_sg, 1)

            def down(k):
                q, n = divmod(k, N0)
                pe.wait_ge(s_glo, k + 1)
                if n == 0 and q:
                    pe.wait_ge(s_acc, 2 * q)
                for m in range(NC):
                    mm = product(pe, PS[:, 5 + m, :], lambda c: w_dn_hi[:, n, P * m:P * m + P],
                                 lambda c: w_dn_lo[:, n, P * m:P * m + P], lambda c: g_hi[:, k % 3, :],
                                 lambda c: g_lo[:, k % 3, :], 1, start=n == 0, stop=False)
                    if n == N0 - 1:
                        mm = pe.matmul(PS[:, 5 + m, :], bst[:, P * m:P * m + P], wt0[:, q % 2, :], start=False, stop=True)
                mm.then_inc(s_dn, 1)

            pe.wait_ge(s_wf, F0_SPLIT)
            for k in range(NK0 + ULAG):
                for q in range(NQ):
                    if k == rows_slot(q):
                        rows(q)
                    for e in range(1, E0, 2):
                        if k == spread_slot(q, e):
                            spread(q, e)
                if k < NK0:
                    up(k)
                for q in range(NQ):
                    if k == gate_slot(q):
                        gate(q)
                if 1 <= k <= NK0:
                    inner(k - 1)
                for q in range(NQ):
                    for e in range(0, E0, 2):
                        if k == spread_slot(q, e):
                            spread(q, e)
                if ULAG <= k:
                    down(k - ULAG)

        @staticmethod
        def scalar(act):
            def keep_spread(k, first):
                for q in range(NQ):
                    for e in range(first, E0, 2):
                        if k == spread_slot(q, e):
                            act.wait_ge(s_wbm, E0 * q + e + 1)
                            if q >= 2:
                                act.wait_ge(s_sp, E0 * (q - 1))
                            act.activation(wb0[:, q % 2, e, :], PS[:, 7, :], ACT.Copy).then_inc(s_wbe, 1)

            for k in range(NK0 + ULAG):
                for q in range(NQ):
                    if k == rows_slot(q):
                        act.wait_ge(s_gT, q + 1)
                        if q >= 2:
                            act.wait_ge(s_dn, N0 * (q - 1))
                        act.activation(wt0[:, q % 2, :], PS[0:96, 7, :], ACT.Copy).then_inc(s_gE, 1)
                if 2 <= k <= NK0 + 1:
                    j = k - 2
                    act.wait_ge(s_sg, j + 1)
                    if j >= 2:
                        act.wait_ge(s_g, j - 1)
                        if sp_count(j - 2):
                            act.wait_ge(s_sp, sp_count(j - 2))
                    act.activation(f_s[:, j % 2, :], PS[:, 4, :], ACT.Silu, bias=b_sw[:, j % N0:j % N0 + 1])\
                       .then_inc(s_si, 1)
                keep_spread(k, 1)
                if FLAG <= k <= NK0 + FLAG - 1:
                    j = k - FLAG
                    act.wait_ge(s_g, j + 1)
                    if j >= 3:
                        act.wait_ge(s_dn, j - 2)
                    act.activation(g_hi[:, j % 3, :], f_g[:, j % 2, :], ACT.Copy).then_inc(s_ghi, 1)
                if k < NK0:
                    act.wait_ge(s_up, k + 1)
                    if k >= 2:
                        act.wait_ge(s_sg, k - 1)
                    act.activation(h_hi[:, k % 2, :], PS[:, k % 4, :], ACT.Identity, bias=b_up[:, k % N0:k % N0 + 1])\
                       .then_inc(s_hhi, 1)
                keep_spread(k, 0)
                q = sum_slot(k - 1)
                if q is not None and q < 2:
                    for c in range(NC):
                        act.wait_ge(s_acc, 2 * q + c + 1)
                        act.activation(xhi[:, c, HALF * (q % 2):HALF * (q % 2) + HALF],
                                       xc_t[:, c, HALF * (q % 2):HALF * (q % 2) + HALF], ACT.Copy).then_inc(s_xh, 1)

        @staticmethod
        def vector(dve):
            dve.memset(wst[:].bitcast(F32), 0.0).then_inc(s_f0c, 1)
            dve.tensor_copy(bst[:], bst_raw[:]).then_inc(s_f0c, 1)
            dve.wait_ge(s_f0c, 2)
            dve.tensor_tensor(bst[64:96, :], bst_raw[64:96, :], bst[64:96, :].bitcast(F32), ALU.subtract)\
               .then_inc(s_f0c, 1)
            dve.wait_ge(s_f0c, 3)

            def gate(q, part):
                r = q // 2
                at = GSTEPS * q
                lj = gl[:].unsqueeze(2).broadcast_to([P, 4, 8, 8])
                li = gl[:].unsqueeze(3).broadcast_to([P, 4, 8, 8])
                if part == 0:
                    dve.wait_ge(s_gm, q + 1)
                    if q:
                        dve.wait_ge(s_gT, q)
                    dve.tensor_tensor(gl[:], PS[:, 7, 0:32].rearrange("p (t e) -> p t e", e=8),
                                      bg_b[:, r, :].unsqueeze(1).broadcast_to([P, 4, 8]), ALU.add).then_inc(s_gs, 1)
                    dve.wait_ge(s_gs, at + 1)
                    dve.tensor_reduce(g_m[:], gl[:], AX.X, ALU.max).then_inc(s_gs, 1)
                    dve.wait_ge(s_gs, at + 2)
                    dve.tensor_tensor(g_w[:], gl[:], g_m[:].unsqueeze(2).broadcast_to([P, 4, 8]), ALU.subtract)\
                       .then_inc(s_gs, 1)
                    dve.tensor_tensor(g_gt[:], lj, li, ALU.is_gt).then_inc(s_gs, 1)
                    dve.tensor_tensor(g_eq[:], lj, li, ALU.is_equal).then_inc(s_gs, 1)
                elif part == 1:
                    dve.wait_ge(s_gs, at + 5)
                    dve.tensor_tensor(g_eq[:], g_eq[:], tri[:].unsqueeze(1).broadcast_to([P, 4, 8, 8]), ALU.mult)\
                       .then_inc(s_gs, 1)
                    dve.wait_ge(s_gs, at + 6)
                    dve.tensor_tensor(g_gt[:], g_gt[:], g_eq[:], ALU.add).then_inc(s_gs, 1)
                    dve.wait_ge(s_gs, at + 7)
                    dve.tensor_reduce(g_rank[:], g_gt[:], AX.X, ALU.add).then_inc(s_gs, 1)
                elif part == 2:
                    dve.wait_ge(s_gs, at + 8)
                    dve.wait_ge(s_gx, 4 * (q + 1))
                    dve.scalar_tensor_tensor(g_w[:], g_rank[:], E0 - 0.5, g_e[:], ALU.is_lt, ALU.mult).then_inc(s_gs, 1)
                    dve.wait_ge(s_gs, at + 9)
                    dve.tensor_reduce(g_m[:], g_w[:], AX.X, ALU.add).then_inc(s_gs, 1)
                    dve.wait_ge(s_gs, at + 10)
                    dve.reciprocal(g_r[:], g_m[:]).then_inc(s_gs, 1)
                    dve.wait_ge(s_gs, at + 11)
                    dve.tensor_tensor(gl[:], g_w[:], g_r[:].unsqueeze(2).broadcast_to([P, 4, 8]), ALU.mult).then_inc(s_gs, 1)
                    dve.wait_ge(s_gs, at + 12)
                    dve.tensor_copy(wst[:, :, 0:8], gl[:]).then_inc(s_gs, 1)
                    dve.wait_ge(s_gs, at + 13)
                    dve.tensor_tensor(wst[:, :, 32:40], gl[:], wst[:, :, 0:8].bitcast(F32), ALU.subtract).then_inc(s_gs, 1)
                    dve.tensor_copy(wst[:, :, 64:72], wst[:, :, 0:8].bitcast(F32)).then_inc(s_gs, 1)

            for k in range(NK0 + ULAG + 1):
                q = sum_slot(k - 1)
                if q is not None:
                    hf = q % 2
                    dve.wait_ge(s_dn, N0 * (q + 1))
                    if q == 0:
                        dve.wait_ge(pre_f0.kept, 4)
                    for c in range(NC):
                        h = slice(HALF * hf, HALF * hf + HALF)
                        dve.scalar_tensor_tensor(xc_t[:, c, h], PS[:, 5 + c, :], b_sd[:, c:c + 1], res_t[:, c, h],
                                                 ALU.add, ALU.add).then_inc(s_acc, 1)
                if FLAG <= k <= NK0 + FLAG - 1:
                    j = k - FLAG
                    n = j % N0
                    if n < 2:
                        dve.wait_ge(s_si, j + 1)
                        w = f_s
                    else:
                        dve.wait_ge(s_sp, sp_count(j))
                        w = f_sw
                    if j >= 2:
                        dve.wait_ge(s_ghi, j - 1)
                        dve.wait_ge(s_glo, j - 1)
                    dve.scalar_tensor_tensor(f_g[:, j % 2, :], PS[:, j % 4, :], b_up[:, n:n + 1], w[:, j % 2, :],
                                             ALU.add, ALU.mult).then_inc(s_g, 1)
                    dve.wait_ge(s_ghi, j + 1)
                    if j >= 3:
                        dve.wait_ge(s_dn, j - 2)
                    dve.tensor_tensor(g_lo[:, j % 3, :], f_g[:, j % 2, :], g_hi[:, j % 3, :].bitcast(F32), ALU.subtract)\
                       .then_inc(s_glo, 1)
                if k < NK0:
                    dve.wait_ge(s_hhi, k + 1)
                    if k >= 2:
                        dve.wait_ge(s_sg, k - 1)
                    dve.scalar_tensor_tensor(h_lo[:, k % 2, :], PS[:, k % 4, :], b_up[:, k % N0:k % N0 + 1],
                                             h_hi[:, k % 2, :].bitcast(F32), ALU.add, ALU.subtract).then_inc(s_hlo, 1)
                q = sum_slot(k - 1)
                if q is not None and q < 2:
                    hf = q % 2
                    for c in range(NC):
                        h = slice(HALF * hf, HALF * hf + HALF)
                        dve.wait_ge(s_xh, 2 * q + c + 1)
                        dve.tensor_tensor(xlo[:, c, h], xc_t[:, c, h], xhi[:, c, h].bitcast(F32), ALU.subtract)\
                           .then_inc(s_xl, 1)
                for q in range(NQ):
                    for part in range(3):
                        if k == gate_part_slot(q, part):
                            gate(q, part)
                if k in A1_SLOTS:
                    attn1_hi(dve, A1_SLOTS.index(k))

        @staticmethod
        def gpsimd(pool):
            pool.wait_ge(post0.x, NT)
            pool.memset(g_base[:], float(np.e)).then_inc(s_gb, 1)
            for k in range(NK0 + 2):
                j = k - 2
                if j >= 0 and j % N0 >= 2:
                    q, n = divmod(j, N0)
                    pool.wait_ge(s_si, j + 1)
                    pool.wait_ge(s_wbe, E0 * q + n - 1)
                    if j >= 2:
                        pool.wait_ge(s_g, j - 1)
                    pool.tensor_tensor(f_sw[:, j % 2, :], f_s[:, j % 2, :], wb0[:, q % 2, n - 2, :], ALU.mult)\
                        .then_inc(s_sp, 1)
                for q in range(NQ):
                    for i in range(4):
                        if k == gate_exp_slot(q, i):
                            pool.wait_ge(s_gb, 1)
                            pool.wait_ge(s_gs, GSTEPS * q + 3)
                            if q:
                                pool.wait_ge(s_gs, GSTEPS * (q - 1) + 9)
                            pool.tensor_tensor(g_e[:, i, :], g_base[:, i, :], g_w[:, i, :], ALU.pow).then_inc(s_gx, 1)
                if k == 6:
                    attn1_load(pool)
                if k - 3 in A1_SLOTS:
                    attn1_lo(pool, A1_SLOTS.index(k - 3))

    def sp_count(k):
        q, n = divmod(k, N0)
        return E0 * q + max(0, n - 1)

    s_a1_ld = sem("attn1_weights_loaded")
    s_a1h = sem("attn1_weights_hi")
    s_a1 = sem("attn1_weights_lo")
    A1 = [(flat(w1q_hi), flat(w1q_lo), 1024), (flat(w1k_hi), flat(w1k_lo), 512), (flat(w1v_hi), flat(w1v_lo), 128),
          (flat(wo_hi), flat(wo_lo), 512)]
    a1_chunks = []
    at = 0
    for hi, lo, n in A1:
        for c in range(0, n, 512):
            w = min(512, n - c)
            a1_chunks.append((at, w, hi[:, c:c + w], lo[:, c:c + w]))
            at += w
    s_rope = sem("rope_loaded")

    A1_SLOTS = (7, 8, 16, 18, 24)
    assert len(A1_SLOTS) == len(a1_chunks)

    def attn1_load(pool):
        pool.wait_ge(s_wf, F0_SPLIT)
        pool.dma_start(stage[:, 0:at], a["w_a1"]).then_inc(s_a1_ld, 16)
        pool.wait_ge(post0.x, NT)
        pool.dma_start(rope[:], a["rope"]).then_inc(s_rope, 16)

    def attn1_hi(dve, n):
        c, w, hi, lo = a1_chunks[n]
        if n == 0:
            dve.wait_ge(s_a1_ld, 16)
            dve.wait_ge(post0.x, NT)
        dve.tensor_copy(hi, stage[:, c:c + w]).then_inc(s_a1h, 1)

    def attn1_lo(pool, n):
        c, w, hi, lo = a1_chunks[n]
        pool.wait_ge(s_a1h, n + 1)
        pool.tensor_tensor(lo, stage[:, c:c + w], hi.bitcast(F32), ALU.subtract).then_inc(s_a1, 1)

    def tokens_again(tag, src_t, wait_src, halves=(0, 1)):
        s_t = sem(tag + "_back")

        class Back(Stage):
            ready = s_t

            @staticmethod
            def half(pe, hf):
                wait_src(pe, hf)
                for t in range(4 * hf, 4 * hf + 4):
                    for c in range(NC):
                        m = pe.transpose(bank_tile(t)[:, P * c:P * c + P], src_t[:, c, P * t:P * t + P], ident[:])
                    m.then_inc(s_t, 1)

            @staticmethod
            def tensor(pe):
                for hf in halves:
                    Back.half(pe, hf)
        return Back

    stages.append(Ffn0)
    back0 = tokens_again("f0", xc_t, lambda pe, hf: pe.wait_ge(s_acc, 2 * NQ))
    stages.append(back0)
    work_f0 = sb("work_f0", [P, NT, D], F32, 70 * K)
    post_f0 = pre1 = norms("to_attn1", work_f0, bank_tile, lambda dve, hf: dve.wait_ge(back0.ready, 4 * hf + 4))
    stages.append(post_f0)

    units1 = [("q", 0, 0), ("q", 0, 1), ("k", 0, 0), ("k", 0, 1), ("q", 1, 0), ("q", 1, 1)]
    part_of = {("q", 0): 0, ("k", 0): 1, ("q", 1): 2}
    split1 = split_parts("qk1", [(parts[part_of[op, m]], hf) for op, m, hf in units1])
    s_qk1 = sem("qk1_product")
    s_cos, s_sin = sem("qk1_cos"), sem("qk1_sin")
    s_v1 = sem("v1_product")
    s_vaug1 = sem("v1_ready")
    s_scr1 = [sem(f"qk1_in_scratch_{n}") for n in ("q", "k", "rest")]
    s_a1c = sem("attn1_constants")

    def store_parts1(sp, m):
        for i, (scr, n) in enumerate(((scr_q, 2), (scr_k, 4)) if m == 0 else ((scr_q, 6),)):
            sp.wait_ge(split1.p3, n)
            sp.dma_start(scr[m].rearrange("s p t -> p s t"), parts[2 * m + i][:])\
              .then_inc(s_scr1[2 if m else i], 16)

    class Project1(Stage):
        @staticmethod
        def tensor(pe):
            pe.wait_ge(s_a1, len(a1_chunks))
            for n, (op, m, hf) in enumerate(units1):
                pe.wait_ge(pre1.features.lo, pre1.features.base + 2 * hf + 2)
                if n >= 2:
                    pe.wait_ge(s_sin, n - 1)
                h = slice(HALF * hf, HALF * hf + HALF)
                for r in range(2):
                    if op == "q":
                        hi, lo = (lambda c: w1q_hi[:, r, c, P * m:P * m + P]), (lambda c: w1q_lo[:, r, c, P * m:P * m + P])
                    else:
                        hi, lo = (lambda c: w1k_hi[:, r, c, :]), (lambda c: w1k_lo[:, r, c, :])
                    mm = product(pe, PS[:, 4 + 2 * (n % 2) + r, :], hi, lo, lambda c: xhi[:, c, h], lambda c: xlo[:, c, h], NC)
                mm.then_inc(s_qk1, 1)
            for n in range(NT):
                t = slice(P * n, P * n + P)
                mm = product(pe, PS[:, 2, 64 * n:64 * n + 64], lambda c: xhi[:, c, t], lambda c: xlo[:, c, t],
                             lambda c: w1v_hi[:, c, :], lambda c: w1v_lo[:, c, :], NC)
            mm.then_inc(s_v1, 1)

        @staticmethod
        def scalar(act):
            for n in range(len(units1)):
                split1.act_first(act, n)
                if n >= 1:
                    split1.act_second(act, n - 1)
            split1.act_second(act, len(units1) - 1)

        @staticmethod
        def gpsimd(pool):
            pool.wait_ge(post_f0.x, NT)
            pool.memset(vaug[:], 1.0).then_inc(s_a1c, 1)
            pool.wait_ge(s_a1c, 1)
            pool.memset(ka[0][96:99, :, :], 1.0).then_inc(s_a1c, 1)
            pool.wait_ge(s_a1c, 2)
            for n in range(len(units1)):
                pool.wait_ge(s_sin, n + 1)
                split1.free(pool, n)
                pool.tensor_tensor(qf[:, n % 2, :], rot[:, n % 2, 0, :], rot[:, n % 2, 1, :], ALU.add)\
                    .then_inc(split1.f, 1)

        @staticmethod
        def vector(dve):
            dve.wait_ge(s_rope, 16)
            for n, (op, m, hf) in enumerate(units1):
                dve.wait_ge(s_qk1, n + 1)
                if n >= 2:
                    dve.wait_ge(split1.f, n - 1)
                h = slice(HALF * hf, HALF * hf + HALF)
                dve.tensor_tensor(rot[:, n % 2, 0, :], PS[:, 4 + 2 * (n % 2), :], rope[:, 0, h], ALU.mult).then_inc(s_cos, 1)
                dve.tensor_tensor(rot[:, n % 2, 1, :], PS[:, 5 + 2 * (n % 2), :], rope[:, 1, h], ALU.mult).then_inc(s_sin, 1)
                if n >= 1:
                    split1.dve_first(dve, n - 1)
                if n >= 2:
                    split1.dve_second(dve, n - 2)
            n = len(units1)
            split1.dve_first(dve, n - 1)
            split1.dve_second(dve, n - 2)
            split1.dve_second(dve, n - 1)
            dve.wait_ge(s_v1, 1)
            dve.wait_ge(s_a1c, 2)
            dve.tensor_copy(vaug[:, :, 0:GROUPS * VW].rearrange("p t (h w) -> p t h w", w=VW)[:, :, :, 0:HD],
                            PS[:, 2, :].rearrange("p (t h w) -> p t h w", t=NT, w=HD)).then_inc(s_vaug1, 1)

        @staticmethod
        def sync(sp):
            store_parts1(sp, 0)

    s_w1_ld = [sem(f"ffn1_weights_loaded{b}") for b in range(2)]
    s_w1h = sem("ffn1_weights_hi")
    s_w1l = sem("ffn1_weights_lo")

    def load_expert(eng, e):
        if e >= 2:
            eng.wait_ge(s_w1l, 3 * (e - 1))
        eng.dma_start(raw1[e % 2][:], a["w_f1"][e]).then_inc(s_w1_ld[e % 2], 16)

    def split_hi(eng, e, piece, on_scalar):
        c = slice(1024 * piece, 1024 * piece + 1024)
        if piece == 0:
            eng.wait_ge(s_w1_ld[e % 2], 16 * (e // 2 + 1))
        src, dst = raw1[e % 2][:, c], w1[e % 2][0][:, piece, :]
        if on_scalar:
            eng.activation(dst, src, ACT.Copy).then_inc(s_w1h, 1)
        else:
            eng.tensor_copy(dst, src).then_inc(s_w1h, 1)

    def split_lo(pool, e, piece):
        c = slice(1024 * piece, 1024 * piece + 1024)
        pool.wait_ge(s_w1h, 3 * e + piece + 1)
        pool.tensor_tensor(w1[e % 2][1][:, piece, :], raw1[e % 2][:, c], w1[e % 2][0][:, piece, :].bitcast(F32),
                           ALU.subtract).then_inc(s_w1l, 1)

    def early_experts(pool, v):
        if v == 0:
            pool.wait_ge(s_a1, len(a1_chunks))
            load_expert(pool, 0)
        elif v == 1:
            for s in s_scr1:
                pool.wait_ge(s, 16)
            load_expert(pool, 1)
        if v >= 2:
            split_hi(pool, (v - 2) // 3, (v - 2) % 3, False)
            split_lo(pool, (v - 2) // 3, (v - 2) % 3)

    stages.append(Project1)
    att1 = attention("att1", True, s_scr1, 16, lambda pe: pe.wait_ge(s_vaug1, 1), GROUPS, store_parts1,
                     EARLY1, early_experts)
    stages.append(att1)
    out1 = out_projection("out1", att1, lambda pe: pe.wait_ge(s_a1, len(a1_chunks)), None)
    stages.append(out1)
    work1 = sb("work1", [P, NT, D], F32, 84 * K)
    post1 = pre_f1 = norms("to_f1", work1, bank_tile, lambda dve, hf: dve.wait_ge(out1.ready, 4 * hf + 4), keep=x1_t)
    stages.append(post1)

    NK1 = E1 * 2 * I1
    DLAG = 2
    s_rwl = sem("router_loaded")
    s_rm = sem("router_logits")
    s_rs = sem("router_step")
    RSTEPS = 17
    s_rT = sem("router_transposed")
    s_rE = sem("router_evacuated")
    s_w1m = sem("f1_weight_broadcast")
    s_w1a, s_w1d = sem("f1_weight_ready_a"), sem("f1_weight_ready_d")
    s_f1c = sem("f1_constants")
    s_ga = sem("f1_gate")
    s_u = sem("f1_up")
    s_f1s = sem("f1_silu")
    s_f1p = sem("f1_silu_weighted")
    s_f1g = sem("f1_g")
    s_f1h = sem("f1_g_hi")
    s_f1l = sem("f1_g_lo")
    s_f1d = sem("f1_down")
    s_y1 = sem("f1_sum_evacuated")

    def gate_up(pe, k):
        e, r = divmod(k, 2 * I1)
        hf, i = divmod(r, I1)
        h = slice(HALF * hf, HALF * hf + HALF)
        if r == 0:
            pe.wait_ge(s_w1l, 3 * e + 2)
        hi, lo = w1[e % 2]
        for j, (s_done, bank, s_used) in enumerate(((s_ga, 4, s_f1s), (s_u, 6, s_f1g))):
            if k >= 2:
                pe.wait_ge(s_used, k - 1)
            product(pe, PS[:, bank + k % 2, :], lambda c: hi[:, j, 512 * c + P * i:512 * c + P * i + P],
                    lambda c: lo[:, j, 512 * c + P * i:512 * c + P * i + P],
                    lambda c: xhi[:, c, h], lambda c: xlo[:, c, h], NC).then_inc(s_done, 1)

    def silu(act, k):
        act.wait_ge(s_ga, k + 1)
        if k >= 3:
            act.wait_ge(s_f1p, k - 2)
        act.activation(m_s[:, k % 3, :], PS[:, 4 + k % 2, :], ACT.Silu).then_inc(s_f1s, 1)

    HEAD = 2

    class Router(Stage):

        @staticmethod
        def sync(sp):
            sp.wait_ge(post1.x, NT)
            sp.dma_start(rw_sb[:], a["w_r1"]).then_inc(s_rwl, 16)

        @staticmethod
        def tensor(pe):
            pe.wait_ge(s_rwl, 16)
            for t in range(NT):
                pe.wait_ge(pre_f1.kept, 2 * (t // 4) + 2)
                for c in range(NC):
                    m = pe.matmul(PS[:, 0, 8 * t:8 * t + 8], x1_t[:, c, P * t:P * t + P], rw_sb[:, c, :],
                                  start=c == 0, stop=c == NC - 1)
            m.then_inc(s_rm, 1)
            pe.wait_ge(pre_f1.features.lo, pre_f1.features.base + 4)
            for k in range(HEAD):
                gate_up(pe, k)
            pe.wait_ge(s_rs, RSTEPS)
            for hf in range(2):
                for i in range(4):
                    m = pe.transpose(PS[0:96, 1 + hf, P * i:P * i + P], wst1[:, 4 * hf + i, :].bitcast(F32), ident[:])
                m.then_inc(s_rT, 1)
            for n in range(2 * E1):
                e, hf = divmod(n, 2)
                pe.wait_ge(s_rE, min(n + 1, 2))
                if n >= 4:
                    k = (n - 4) // 2 + 1
                    pe.wait_ge(s_w1a if n % 2 == 0 else s_w1d, k)
                pe.matmul(PS[:, n % 4, :], sel[:, e, :], wt1[:, HALF * hf:HALF * hf + HALF], start=True, stop=True)\
                  .then_inc(s_w1m, 1)

        @staticmethod
        def scalar(act):
            act.wait_ge(s_rs, 3)
            act.activation(r_e[:], r_x[:], ACT.Exp).then_inc(s_rs, 1)
            for k in range(HEAD):
                silu(act, k)
            for hf in range(2):
                act.wait_ge(s_rT, hf + 1)
                act.activation(wt1[:, HALF * hf:HALF * hf + HALF], PS[0:96, 1 + hf, :], ACT.Copy).then_inc(s_rE, 1)
            for n in range(0, 2 * E1, 2):
                act.wait_ge(s_w1m, n + 1)
                act.activation(wb1[:, n // 2, 0:HALF], PS[:, n % 4, :], ACT.Copy).then_inc(s_w1a, 1)

        @staticmethod
        def vector(dve):
            st = Steps(s_rs)
            dve.memset(wst1[:].bitcast(F32), 0.0).then_inc(s_f1c, 1)
            dve.wait_ge(s_rm, 1)
            dve.tensor_copy(r_l[:], PS[:, 0, 0:64].rearrange("p (t e) -> p t e", e=8)).then_inc(s_rs, 1)
            st.wait(dve, 1)
            dve.tensor_reduce(r_m[:], r_l[:], AX.X, ALU.max).then_inc(s_rs, 1)
            st.wait(dve, 1)
            dve.tensor_tensor(r_x[:], r_l[:], r_m[:].unsqueeze(2).broadcast_to([P, NT, 8]), ALU.subtract)\
               .then_inc(s_rs, 1)
            st.wait(dve, 2)
            dve.tensor_reduce(r_m[:], r_e[:], AX.X, ALU.add).then_inc(s_rs, 1)
            st.wait(dve, 1)
            dve.reciprocal(r_s[:], r_m[:]).then_inc(s_rs, 1)
            st.wait(dve, 1)
            dve.tensor_tensor(r_p[:], r_e[:], r_s[:].unsqueeze(2).broadcast_to([P, NT, 8]), ALU.mult).then_inc(s_rs, 1)
            st.wait(dve, 1)
            lj = r_p[:].unsqueeze(2).broadcast_to([P, NT, 8, 8])
            stands_before(dve, st, r_p, r_gt, r_eq, NT)
            dve.tensor_tensor(r_gt[:], r_gt[:], lj, ALU.mult).then_inc(s_rs, 1)
            st.wait(dve, 1)
            dve.tensor_reduce(r_x[:], r_gt[:], AX.X, ALU.add).then_inc(s_rs, 1)
            st.wait(dve, 1)
            dve.scalar_tensor_tensor(r_w[:], r_x[:], TOP_P, r_p[:], ALU.is_le, ALU.mult).then_inc(s_rs, 1)
            st.wait(dve, 1)
            dve.wait_ge(s_f1c, 1)
            stack_weights(dve, st, r_w, wst1)
            assert st.at == RSTEPS, st.at
            for n in range(1, 2 * E1, 2):
                dve.wait_ge(s_w1m, n + 1)
                dve.tensor_copy(wb1[:, n // 2, HALF:T], PS[:, n % 4, :]).then_inc(s_w1d, 1)

    back1 = tokens_again("f1", y1_t, lambda pe, hf: pe.wait_ge(s_y1, 2 * hf + 2), halves=(1,))

    class Ffn1(Stage):
        @staticmethod
        def tensor(pe):
            def down(k):
                e, r = divmod(k, 2 * I1)
                hf, i = divmod(r, I1)
                hi, lo = w1[e % 2]
                if k == 0:
                    pe.wait_ge(s_w1a, E1)
                    pe.wait_ge(s_w1d, E1)
                if r == 0:
                    pe.wait_ge(s_w1l, 3 * e + 3)
                pe.wait_ge(s_f1l, k + 1)
                for m in range(NC):
                    mm = product(pe, PS[:, 2 * hf + m, :], lambda c: hi[:, 2, D * i + P * m:D * i + P * m + P],
                                 lambda c: lo[:, 2, D * i + P * m:D * i + P * m + P],
                                 lambda c: m_ghi[:, k % 3, :], lambda c: m_glo[:, k % 3, :], 1,
                                 start=e == 0 and i == 0, stop=e == E1 - 1 and i == I1 - 1)
                mm.then_inc(s_f1d, 1)

            for k in range(NK1 + DLAG):
                if HEAD <= k < NK1:
                    gate_up(pe, k)
                if k == NK1 + DLAG - 1:
                    pe.wait_ge(s_f1s, NK1)
                    back1.half(pe, 0)
                if k >= DLAG:
                    down(k - DLAG)

        @staticmethod
        def scalar(act):
            def keep_sums(hf):
                act.wait_ge(s_f1d, NK1 - (I1 if hf == 0 else 0))
                for c in range(NC):
                    act.activation(y1_t[:, c, HALF * hf:HALF * hf + HALF], PS[:, 2 * hf + c, :], ACT.Copy)\
                       .then_inc(s_y1, 1)

            for k in range(NK1 + 1):
                if HEAD <= k < NK1:
                    silu(act, k)
                if k == NK1 - 1:
                    keep_sums(0)
                if k >= 1:
                    j = k - 1
                    act.wait_ge(s_f1g, j + 1)
                    if j >= 3:
                        act.wait_ge(s_f1d, j - 2)
                    act.activation(m_ghi[:, j % 3, :], m_g[:, j % 2, :], ACT.Copy).then_inc(s_f1h, 1)
                e, r = divmod(k, 2 * I1)
                if e + 1 < E1 and e >= 1 and r in (3, 5, 7):
                    piece = (r - 3) // 2
                    act.wait_ge(s_f1d, 2 * I1 * e)
                    split_hi(act, e + 1, piece, True)
            keep_sums(1)

        @staticmethod
        def vector(dve):
            for k in range(NK1):
                dve.wait_ge(s_u, k + 1)
                dve.wait_ge(s_f1p, k + 1)
                if k >= 2:
                    dve.wait_ge(s_f1h, k - 1)
                    dve.wait_ge(s_f1l, k - 1)
                dve.tensor_tensor(m_g[:, k % 2, :], PS[:, 6 + k % 2, :], m_sw[:, k % 3, :], ALU.mult).then_inc(s_f1g, 1)
                dve.wait_ge(s_f1h, k + 1)
                if k >= 3:
                    dve.wait_ge(s_f1d, k - 2)
                dve.tensor_tensor(m_glo[:, k % 3, :], m_g[:, k % 2, :], m_ghi[:, k % 3, :].bitcast(F32), ALU.subtract)\
                   .then_inc(s_f1l, 1)

        @staticmethod
        def gpsimd(pool):
            for k in range(NK1):
                e, r = divmod(k, 2 * I1)
                if r == 2 and e == 0:
                    load_expert(pool, 2)
                if r % I1 == 0:
                    pool.wait_ge(s_w1d if r else s_w1a, e + 1)
                if r == 0 and 1 <= e and e + 2 < E1:
                    load_expert(pool, e + 2)
                pool.wait_ge(s_f1s, k + 1)
                if k >= 3:
                    pool.wait_ge(s_f1g, k - 2)
                pool.tensor_tensor(m_sw[:, k % 3, :], m_s[:, k % 3, :],
                                   wb1[:, e, HALF * (r // I1):HALF * (r // I1) + HALF], ALU.mult).then_inc(s_f1p, 1)
                if e + 1 < E1 and e >= 1 and r in (3, 5, 7):
                    split_lo(pool, e + 1, (r - 3) // 2)

    stages.append(Router)
    stages.append(Ffn1)
    stages.append(back1)
    work_f1 = sb("work_f1", [P, NT, D], F32, 84 * K)
    post_f1 = norms("to_out", work_f1, bank_tile, lambda dve, hf: dve.wait_ge(back1.ready, 4 * hf + 4),
                    transposed=False)
    stages.append(post_f1)
    last_x = post_f1.x

    s_out = sem("out_stored")

    class Store(Stage):
        @staticmethod
        def sync(sp):
            for hf in range(2):
                sp.wait_ge(last_x, 4 * hf + 4)
                sp.dma_start(out.rearrange("(t p) d -> p t d", p=P)[:, 4 * hf:4 * hf + 4, :],
                             x_res[:, 4 * hf:4 * hf + 4, :]).then_inc(s_out, 16)
            sp.wait_ge(s_out, 32)

    stages.append(Store)

    block = ctx.enter_context(nc.Block())

    @block.sync
    def _(sp):
        for stage_of in stages:
            stage_of.sync(sp)

    @block.gpsimd
    def _(pool):
        for stage_of in stages:
            stage_of.gpsimd(pool)

    @block.scalar
    def _(act):
        for stage_of in stages:
            stage_of.scalar(act)

    @block.vector
    def _(dve):
        for stage_of in stages:
            stage_of.vector(dve)

    @block.tensor
    def _(pe):
        for stage_of in stages:
            stage_of.tensor(pe)


def host(inputs):
    f = lambda n: np.ascontiguousarray(np.asarray(inputs[n]))
    A = "L0_attn_"
    d = {"x": f(A + "x").reshape(T, D)}
    d["w_attn0"] = np.stack([f(A + "W" + m).T for m in "qkvo"])
    d["lora"] = np.stack([np.stack([f(A + "A" + m).T for m in "qkvo"]), np.stack([f(A + "B" + m) for m in "qkvo"])])
    d["bqk"] = np.stack([f(A + "b" + m).reshape(NC, P).T for m in "qk"], axis=1)
    d["bvo"] = np.stack([f(A + "bv"), f(A + "bo")])
    d["ident"] = np.eye(P, dtype=np.float32)
    i = np.arange(P)
    later = (i[None, :] > i[:, None])
    d["masks"] = np.ascontiguousarray(np.stack([np.where(later, BIG, 0), np.where(later.T, BIG, 0)], 1).astype(np.float32))
    j = np.arange(8)
    d["tri"] = np.ascontiguousarray(np.broadcast_to((j[None, :] < j[:, None]).astype(np.float32), (P, 8, 8)))
    chunk = lambda w: w.reshape(-1, P, w.shape[-1]).transpose(1, 0, 2)
    F = "L0_ffn_"
    wsu, wsd = f(F + "Wsu"), f(F + "Wsd")
    up = [wsu[:, :P], wsu[:, P:]] + list(f(F + "Wup"))
    sw = [f(F + "Wsa")] * 2 + list(f(F + "Wsw"))
    dn = [wsd[:P], wsd[P:]] + list(f(F + "Wdn"))
    d["w_f0"] = np.concatenate([np.stack([chunk(w) for w in up], 1).reshape(P, -1),
                                np.stack(sw, 1).reshape(P, -1), np.stack(dn, 1).reshape(P, -1)], 1)
    d["b_up0"] = np.concatenate([f(F + "bsu").reshape(2, P), f(F + "bup")]).T
    d["b_sw0"] = np.concatenate([np.stack([f(F + "bsa")] * 2), f(F + "bsw")]).T
    d["b_sd0"] = f(F + "bsd").reshape(NC, P).T
    d["b_g0"] = f(F + "bg")[None]
    b = np.zeros((96, D), np.float32)
    for r in (0, 32, 64):
        b[r:r + E0] = f(F + "bdn")
    d["b_dn0"] = b
    d["w_g0"] = f(F + "Wg").reshape(ROUNDS, NC, P, 8).transpose(2, 0, 1, 3)
    d["sel"] = np.zeros((96, 8, P), np.float32)
    for e in range(8):
        d["sel"][[e, 32 + e], e] = 1
    B = "L1_attn_"
    turn = np.arange(D) // HD * HD + (np.arange(D) + HD // 2) % HD
    wq, wk, wv, wo = (f(B + "W" + m) for m in "qkvo")
    wk2 = np.concatenate([wk, wk], 1)
    cat = [wq, wq[:, turn], wk2, wk2[:, turn[:P]], wv, wo]
    d["w_a1"] = np.concatenate([chunk(w).reshape(P, -1) for w in cat], 1)
    inv = np.power(np.float32(10000), (np.float32(-2) * np.arange(HD // 2, dtype=np.float32) / np.float32(HD)))
    ang = np.arange(T, dtype=np.float32)[:, None] * inv[None].astype(np.float32)
    cos, sin = np.tile(np.cos(ang), (1, 2)).T, np.tile(np.sin(ang), (1, 2)).T
    sin = np.concatenate([-sin[:HD // 2], sin[HD // 2:]])
    d["rope"] = np.stack([np.tile(cos, (P // HD, 1)), np.tile(sin, (P // HD, 1))], 1).astype(np.float32)
    M = "L1_ffn_"
    d["w_r1"] = chunk(f(M + "router_w").T)
    gw, uw, dw = f(M + "gate_w"), f(M + "up_w"), f(M + "down_w")
    d["w_f1"] = np.stack([np.concatenate([chunk(gw[e].T).reshape(P, -1), chunk(uw[e].T).reshape(P, -1),
                                          chunk(dw[e].T).reshape(P, -1)], 1) for e in range(E1)])
    return {k: np.ascontiguousarray(v) for k, v in d.items()}


def kernel(**inputs):
    import concourse.bacc as _bacc
    from concourse.bass_utils import run_bass_kernel_spmd as _run

    arrays = host(inputs)
    nc = _bacc.Bacc("TRN2", target_bir_lowering=False, num_devices=1)
    aps = {k: nc.dram_tensor("in_" + k, v.shape, mybir.dt.from_np(v.dtype), kind="ExternalInput").ap()
           for k, v in arrays.items()}
    out = nc.dram_tensor("out_x", [T, D], F32, kind="ExternalOutput").ap()
    program(nc, aps, out)
    r = _run(nc, [{"in_" + k: v for k, v in arrays.items()}], core_ids=[0])
    return r.results[0]["out_x"].reshape(1, T, D)
```
